# Optimizing a Trainium2 kernel written in Bass

```python
import numpy as np
import jax
import jax.numpy as jnp

def _softmax(x, axis=-1):
    return jax.nn.softmax(x, axis=axis)
def _gelu(x):
    return jax.nn.gelu(x, approximate=True)
def _silu(x):
    return jax.nn.silu(x)
def _sigmoid(x):
    return jax.nn.sigmoid(x)
def _layernorm(x, axis=-1, eps=1e-5):
    m = jnp.mean(x, axis=axis, keepdims=True)
    v = jnp.var(x, axis=axis, keepdims=True)
    return (x - m) / jnp.sqrt(v + eps)
def _scatter_add(tgt, idx, src, axis=0):
    return tgt.at[idx].add(src)
def _segment_sum(src, seg, n):
    return jax.ops.segment_sum(src, seg, n)

kernel_name = 'mk_adj_resnorm_d4_adj_256_eb247a'

def setup_inputs(seed: int = 0):
    np.random.seed(seed)
    _w = jnp.asarray
    def _rec_inputs():
        import jax
        import jax.numpy as jnp
        _gk = jax.random.key(seed)
        x = -0.0002928 + 1 * jax.random.normal(jax.random.fold_in(_gk, 1), (16, 1024, 256), jnp.float32)
        _a = jax.random.bernoulli(jax.random.fold_in(_gk, 2), 0.0078125, (16, 1024, 1024))
        _a = jnp.logical_or(_a, jnp.swapaxes(_a, -1, -2))
        _a = jnp.logical_or(_a, jnp.eye(1024, dtype=bool))
        _af = _a.astype(jnp.float32)
        _af = _af * jax.random.uniform(jax.random.fold_in(_gk, 3), (16, 1024, 1024), jnp.float32, 0.05, 0.999994)
        adj = _af
        _nm = jnp.ones((16, 1024), dtype=bool)
        nodemask = jnp.where(_nm, 1.0, 0.0).astype(jnp.float32)
        return x, adj, nodemask
    x, adj, nodemask = _rec_inputs()
    def _L0_gnn_setup():
        import jax, jax.numpy as jnp
        import numpy as np
        EPS = 1e-08
        key = jax.random.key(seed)
        kH, kA, kW = jax.random.split(key, 3)
        B, N, IN, OUT = (32, 512, 256, 256)
        H = jax.random.normal(kH, (B, N, IN), dtype=jnp.float32)
        A = jax.random.uniform(kA, (B, N, N), dtype=jnp.float32)
        mask = jnp.ones((B, N), dtype=jnp.float32)
        W = jax.random.normal(kW, (OUT, IN), dtype=jnp.float32) * (1.0 / np.sqrt(IN))
        b = jnp.zeros((OUT,), dtype=jnp.float32)
        return {'H': H, 'A': A, 'mask': mask, 'W': W, 'b': b}
    _L0_gnn_all = _L0_gnn_setup()
    _L0_gnn_in = {k: v for k, v in _L0_gnn_all.items() if k in ('W', 'b', )}
    del _L0_gnn_all

    def _L1_gnn_setup():
        import jax, jax.numpy as jnp
        import numpy as np
        SPARSITY = 0.01

        def quantize(weight, s):
            pos = (weight > s).astype(weight.dtype)
            neg = (weight < -s).astype(weight.dtype)
            return (pos - neg) * s
        key = jax.random.key(seed)
        k1, k2, k3 = jax.random.split(key, 3)
        B, N, Din, Dout = (8, 2048, 256, 256)
        x = jax.random.normal(k1, (B, N, Din), dtype=jnp.float32)
        adj = jax.random.uniform(k2, (B, N, N), dtype=jnp.float32)
        limit = float(np.sqrt(6.0 / (Din + Dout)))
        weight = jax.random.uniform(k3, (Din, Dout), dtype=jnp.float32, minval=-limit, maxval=limit)
        bias = jnp.zeros((Dout,), dtype=jnp.float32)
        return {'x': x, 'adj': adj, 'weight': weight, 'bias': bias}
    _L1_gnn_all = _L1_gnn_setup()
    _L1_gnn_in = {k: v for k, v in _L1_gnn_all.items() if k in ('weight', 'bias', )}
    del _L1_gnn_all

    def _L2_gnn_setup():
        import jax, jax.numpy as jnp
        import numpy as np
        GROUPS = [list(range(25)), [0, 1, 2, 3, 4, 5, 6, 7, 8], [0, 9, 10, 11, 12, 13, 14], [6, 7, 8, 12, 13, 14], [3, 4, 5, 9, 10, 11]]
        B, N, D_IN, D_HID = (8192, 25, 256, 512)

        def _graph_conv(x, adj, W, b):
            n = adj.shape[-1]
            A = adj + jnp.eye(n, dtype=adj.dtype)
            deg = jnp.sum(A, axis=-1)
            deg_safe = jnp.where(deg == 0, 1.0, deg)
            dinv = jnp.where(deg == 0, 0.0, deg_safe ** (-0.5))
            norm_adj = dinv[:, :, None] * A * dinv[:, None, :]
            support = jnp.einsum('bnd,de->bne', x, W)
            out = jnp.einsum('bnm,bme->bne', norm_adj, support) + b
            return jax.nn.relu(out)
        key = jax.random.key(seed)
        ks = jax.random.split(key, 7)
        s1 = float(np.sqrt(6.0 / (D_IN + D_HID)))
        s2 = float(np.sqrt(6.0 / (D_HID + D_IN)))
        return {'x': jax.random.normal(ks[0], (B, N, D_IN), dtype=jnp.float32), 'adj': jax.random.uniform(ks[1], (B, N, N), dtype=jnp.float32), 'W1': jax.random.uniform(ks[2], (5, D_IN, D_HID), jnp.float32, -s1, s1), 'b1': jnp.zeros((5, D_HID), dtype=jnp.float32), 'W2': jax.random.uniform(ks[3], (5, D_HID, D_IN), jnp.float32, -s2, s2), 'b2': jnp.zeros((5, D_IN), dtype=jnp.float32), 'fusion_w': jnp.ones((5,), dtype=jnp.float32)}
    _L2_gnn_all = _L2_gnn_setup()
    _L2_gnn_in = {k: v for k, v in _L2_gnn_all.items() if k in ('W1', 'b1', 'W2', 'b2', 'fusion_w', )}
    del _L2_gnn_all

    def _L3_gnn_setup():
        import jax, jax.numpy as jnp
        import numpy as np
        B, N, D, H = (8, 2048, 256, 1024)
        RMS_EPS = 1e-06

        def _rmsnorm(h, w, eps=RMS_EPS):
            var = jnp.mean(jnp.square(h), axis=-1, keepdims=True)
            return h * jax.lax.rsqrt(var + eps) * w
        key = jax.random.key(seed)
        ks = jax.random.split(key, 5)
        x = jax.random.normal(ks[0], (B, N, D), dtype=jnp.float32)
        adjacency = jax.random.uniform(ks[1], (B, N, N), dtype=jnp.float32)
        epsilon = jnp.zeros((), dtype=jnp.float32)
        W1 = jax.random.normal(ks[2], (D, H), dtype=jnp.float32) * (1.0 / np.sqrt(D))
        b1 = jnp.zeros((H,), dtype=jnp.float32)
        rms_weight = jnp.ones((H,), dtype=jnp.float32)
        W2 = jax.random.normal(ks[3], (H, D), dtype=jnp.float32) * (1.0 / np.sqrt(H))
        b2 = jnp.zeros((D,), dtype=jnp.float32)
        return {'x': x, 'adjacency': adjacency, 'epsilon': epsilon, 'W1': W1, 'b1': b1, 'rms_weight': rms_weight, 'W2': W2, 'b2': b2}
    _L3_gnn_all = _L3_gnn_setup()
    _L3_gnn_in = {k: v for k, v in _L3_gnn_all.items() if k in ('epsilon', 'W1', 'b1', 'rms_weight', 'W2', 'b2', )}
    del _L3_gnn_all

    return {
        "x": x,
        "adj": adj,
        "nodemask": nodemask,
        "L0_gnn_W": _L0_gnn_in["W"],
        "L0_gnn_b": _L0_gnn_in["b"],
        "L1_gnn_weight": _L1_gnn_in["weight"],
        "L1_gnn_bias": _L1_gnn_in["bias"],
        "L2_gnn_W1": _L2_gnn_in["W1"],
        "L2_gnn_b1": _L2_gnn_in["b1"],
        "L2_gnn_W2": _L2_gnn_in["W2"],
        "L2_gnn_b2": _L2_gnn_in["b2"],
        "L2_gnn_fusion_w": _L2_gnn_in["fusion_w"],
        "L3_gnn_epsilon": _L3_gnn_in["epsilon"],
        "L3_gnn_W1": _L3_gnn_in["W1"],
        "L3_gnn_b1": _L3_gnn_in["b1"],
        "L3_gnn_rms_weight": _L3_gnn_in["rms_weight"],
        "L3_gnn_W2": _L3_gnn_in["W2"],
        "L3_gnn_b2": _L3_gnn_in["b2"],
    }

def reference(x, adj, nodemask, L0_gnn_W, L0_gnn_b, L1_gnn_weight, L1_gnn_bias, L2_gnn_W1, L2_gnn_b1, L2_gnn_W2, L2_gnn_b2, L2_gnn_fusion_w, L3_gnn_epsilon, L3_gnn_W1, L3_gnn_b1, L3_gnn_rms_weight, L3_gnn_W2, L3_gnn_b2):
    import jax
    import jax.numpy as jnp
    def _L0_gnn_ref(H, A, mask, W, b):
        import jax, jax.numpy as jnp
        import numpy as np
        EPS = 1e-08
        N = A.shape[-1]
        A_hat = A + jnp.eye(N, dtype=A.dtype)
        deg = A_hat.sum(axis=-1)
        dis = (deg + EPS) ** (-0.5)
        A_norm = dis[:, :, None] * A_hat * dis[:, None, :]
        H_lin = jnp.einsum('bni,oi->bno', H, W) + b
        out = jnp.einsum('bnm,bmo->bno', A_norm, H_lin)
        out = out * mask[:, :, None]
        return jax.nn.relu(out)

    def _L1_gnn_ref(x, adj, weight, bias):
        import jax, jax.numpy as jnp
        import numpy as np
        SPARSITY = 0.01

        def quantize(weight, s):
            pos = (weight > s).astype(weight.dtype)
            neg = (weight < -s).astype(weight.dtype)
            return (pos - neg) * s
        dw = quantize(weight, SPARSITY)
        support = jnp.einsum('bni,io->bno', x, dw)
        out = jnp.einsum('bnm,bmo->bno', adj, support) + bias
        return jax.nn.relu(out)

    def _L2_gnn_ref(x, adj, W1, b1, W2, b2, fusion_w):
        import jax, jax.numpy as jnp
        import numpy as np
        GROUPS = [list(range(25)), [0, 1, 2, 3, 4, 5, 6, 7, 8], [0, 9, 10, 11, 12, 13, 14], [6, 7, 8, 12, 13, 14], [3, 4, 5, 9, 10, 11]]
        B, N, D_IN, D_HID = (8192, 25, 256, 512)

        def _graph_conv(x, adj, W, b):
            n = adj.shape[-1]
            A = adj + jnp.eye(n, dtype=adj.dtype)
            deg = jnp.sum(A, axis=-1)
            deg_safe = jnp.where(deg == 0, 1.0, deg)
            dinv = jnp.where(deg == 0, 0.0, deg_safe ** (-0.5))
            norm_adj = dinv[:, :, None] * A * dinv[:, None, :]
            support = jnp.einsum('bnd,de->bne', x, W)
            out = jnp.einsum('bnm,bme->bne', norm_adj, support) + b
            return jax.nn.relu(out)
        norm_w = jax.nn.softmax(fusion_w)
        fused = jnp.zeros_like(x)
        for g, idx_list in enumerate(GROUPS):
            idx = jnp.asarray(idx_list)
            x_g = x[:, idx, :]
            adj_g = adj[:, idx][:, :, idx]
            h = _graph_conv(x_g, adj_g, W1[g], b1[g])
            out_g = _graph_conv(h, adj_g, W2[g], b2[g])
            fused = fused.at[:, idx, :].add(norm_w[g] * out_g)
        return fused

    def _L3_gnn_ref(x, adjacency, epsilon, W1, b1, rms_weight, W2, b2):
        import jax, jax.numpy as jnp
        import numpy as np
        B, N, D, H = (8, 2048, 256, 1024)
        RMS_EPS = 1e-06

        def _rmsnorm(h, w, eps=RMS_EPS):
            var = jnp.mean(jnp.square(h), axis=-1, keepdims=True)
            return h * jax.lax.rsqrt(var + eps) * w
        neighbor_sum = jnp.einsum('bnm,bmd->bnd', adjacency, x)
        agg = epsilon * x + neighbor_sum
        h = jnp.einsum('bnd,dh->bnh', agg, W1) + b1
        h = jax.nn.silu(_rmsnorm(h, rms_weight))
        out = jnp.einsum('bnh,hd->bnd', h, W2) + b2
        return out

    x = _layernorm(x + _L0_gnn_ref(x, adj, nodemask, L0_gnn_W, L0_gnn_b), axis=-1)
    x = _layernorm(x + _L1_gnn_ref(x, adj, L1_gnn_weight, L1_gnn_bias), axis=-1)
    x = _layernorm(x + _L2_gnn_ref(x, adj, L2_gnn_W1, L2_gnn_b1, L2_gnn_W2, L2_gnn_b2, L2_gnn_fusion_w), axis=-1)
    x = _layernorm(x + _L3_gnn_ref(x, adj, L3_gnn_epsilon, L3_gnn_W1, L3_gnn_b1, L3_gnn_rms_weight, L3_gnn_W2, L3_gnn_b2), axis=-1)
    return x


_drawn_inputs = setup_inputs


def setup_inputs(seed=0):
    import zlib

    import numpy as np

    out = dict(_drawn_inputs(seed))
    spreads = {'L0_gnn_b': (0.0, 0.1),
     'L1_gnn_bias': (0.0, 0.1),
     'L2_gnn_b1': (0.0, 2.0),
     'L2_gnn_b2': (0.0, 2.0),
     'L2_gnn_fusion_w': (1.0, 0.6),
     'L3_gnn_b1': (0.0, 0.346),
     'L3_gnn_rms_weight': (1.0, 0.2),
     'L3_gnn_b2': (0.0, 0.1)}
    factors = {'L2_gnn_W1': 4.272, 'L2_gnn_W2': 3.617}
    for name, (base, spread) in spreads.items():
        noise = np.random.default_rng([zlib.crc32(name.encode()), seed]).standard_normal(out[name].shape)
        drawn = base * np.exp(spread * noise) if base else spread * noise
        out[name] = jnp.asarray(drawn.astype(out[name].dtype))
    for name, factor in factors.items():
        out[name] = (out[name] * factor).astype(out[name].dtype)
    return out
```

```python
from contextlib import ExitStack

import numpy as np

import concourse.bass as bass
from concourse import mybir
from concourse.alu_op_type import AluOpType as ALU

F32 = mybir.dt.float32
F32R = mybir.dt.float32r
ACT = mybir.ActivationFunctionType

P = 128
LN_EPS = 1e-5
DEG_EPS = 1e-8
QUANT = 0.01
RMS_EPS = 1e-6
GROUPS = [list(range(25)), [0, 1, 2, 3, 4, 5, 6, 7, 8], [0, 9, 10, 11, 12, 13, 14],
          [6, 7, 8, 12, 13, 14], [3, 4, 5, 9, 10, 11]]
NODES = 25


def f32(ap):
    return ap.bitcast(F32)


def split_matmuls(nc, out, w_hi, w_lo, m_hi, m_lo, first, last, group=True):
    nc.tensor.matmul(out, w_hi, m_hi, start=first, stop=False, skip_group_check=not group)
    nc.tensor.matmul(out, w_hi, m_lo, start=False, stop=False, skip_group_check=not group)
    return nc.tensor.matmul(out, w_lo, m_hi, start=False, stop=last, skip_group_check=not group)


def part1(nc, x, adj, nodemask, w0t, b0, w1, b1, eps, eye, mixed, x3, nbr25, x2head):
    B, N, D = x.shape
    T = N // P
    DT = D // P
    H = N // 2
    TH = T // 2
    R = 4
    assert H == 512 and D == 256 and T == 8

    with ExitStack() as ctx:
        def sb(name, shape, dt=F32):
            return ctx.enter_context(nc.sbuf_tensor(name, shape, dt))

        def ps(name, shape):
            return ctx.enter_context(nc.psum_tensor(name, shape, F32))

        def sem(name):
            return ctx.enter_context(nc.semaphore(name))

        at_hi, at_lo = sb("at_hi", [P, T, N], F32R), sb("at_lo", [P, T, N], F32R)
        a_rows = sb("a_rows", [P, T, N])
        x_in = sb("x_in", [P, T, D])
        xres = sb("xres", [P, T, D])
        sup = sb("sup", [P, T, D])
        mv0_hi, mv0_lo = sb("mv0_hi", [P, T * D], F32R), sb("mv0_lo", [P, T * D], F32R)
        x1_hi, x1_lo = sb("x1_hi", [P, T, D], F32R), sb("x1_lo", [P, T, D], F32R)
        x3_hi, x3_lo = sb("x3_hi", [P, T, D], F32R), sb("x3_lo", [P, T, D], F32R)
        mix_sb = sb("mix_sb", [P, 2 * DT, H])
        xt_hi, xt_lo = sb("xt_hi", [P, 2, DT, P], F32R), sb("xt_lo", [P, 2, DT, P], F32R)
        row = sb("row", [P, R, D])
        diag = sb("diag", [P, T, P])
        junk = sb("junk", [P, N], mybir.dt.bfloat16)
        head = sb("head", [NODES, D])
        ident, epsi = sb("ident", [P, P]), sb("epsi", [P, P])
        w0_hi, w0_lo = sb("w0_hi", [P, DT, D], F32R), sb("w0_lo", [P, DT, D], F32R)
        dw = sb("dw", [P, DT, D], F32R)
        b0_bc, b1_bc = sb("b0_bc", [P, D]), sb("b1_bc", [P, D])
        masks = sb("masks", [P, B * T])
        degs, dis, dism = sb("degs", [P, T]), sb("dis", [P, T]), sb("dism", [P, T])
        minus_half = sb("minus_half", [P, T])
        stats = sb("stats", [P, 4, 6])
        mean_var = sb("mean_var", [P, 3, T, 2])
        var_eps, rstd = sb("var_eps", [P, 3, T]), sb("rstd", [P, 3, T])
        eps_sb, spacer, spacer_p = sb("eps_sb", [P, 1]), sb("spacer", [P, 1]), sb("spacer_p", [P, 1])
        w_stage = sup
        m_stage = row[:, 0, 0:P]

        tr = [ps(f"tr{i}", [P, H]) for i in range(2)]
        nt = [ps(f"nt{i}", [P, D]) for i in range(2)]
        acc = [ps(f"acc{i}", [P, H]) for i in range(4)]

        names = ["consts", "a_loaded0", "a_loaded1", "a_loaded2", "a_loaded3", "x_loaded", "head_out", "nbr_out", "x3_out", "mix_out",
                 "setup_v", "setup_p", "setup_a", "setup_t",
                 "transposed", "at_hi_ok", "at_lo_ok", "xt_hi_ok", "xt_lo_ok",
                 "sup_psum", "sup_ok", "mv_hi_ok", "mv_lo_ok", "deg_sum", "deg_ok", "dis_pow", "dism_ok",
                 "m0_psum", "row0_ok", "relu0_ok", "y0_ok", "st0_a", "st0_b", "var0_ok", "pow0_ok",
                 "x1_ok", "x1_hi_ok", "x1_lo_ok",
                 "z_psum", "z_hi_ok", "z_lo_ok", "diag_a", "diag_ok", "at_hi_eps", "at_lo_eps",
                 "m1_psum", "row1_ok", "relu1_ok", "y1_ok", "st1_a", "st1_b", "var1_ok", "pow1_ok",
                 "x2_ok", "head_ok", "st2_a", "st2_b", "var2_ok", "pow2_ok", "x3_ok", "x3_hi_ok",
                 "x3_lo_ok", "x3_lo0", "mix_psum", "mix_ok"]
        S = {n: sem("p1_" + n) for n in names}

        def diag_tiles(at, half):
            flat = at[:].rearrange("p k n -> p (k n)")
            even = flat[:, 0:(T - 1) * (N + P)].rearrange("p (k w) -> p k w", k=T - 1)
            if half == 0:
                return [(even[:, 0:TH, 0:P], slice(0, TH))]
            return [(even[:, TH:T - 1, 0:P], slice(TH, T - 1)),
                    (at[:, T - 1:T, (T - 1) * P:T * P], slice(T - 1, T))]

        block = ctx.enter_context(nc.Block("part1"))

        a_v = adj.rearrange("b (t p) m -> b p t m", p=P)
        x_v = x.rearrange("b (t p) d -> b p t d", p=P)
        x3_v = x3.rearrange("b (t p) d -> b p t d", p=P)

        @block.sync
        def _(sp):
            sp.dma_start(ident[:], eye).then_inc(S["consts"], 16)
            sp.dma_start(w_stage[:, 0:DT, :], w0t.rearrange("(k p) o -> p k o", p=P)).then_inc(S["consts"], 16)
            sp.dma_start(w_stage[:, DT:2 * DT, :], w1.rearrange("(k p) o -> p k o", p=P)).then_inc(S["consts"], 16)
            sp.dma_start(b0_bc[:], b0.rearrange("(a d) -> a d", a=1).broadcast_to([P, D])).then_inc(S["consts"], 16)
            sp.dma_start(b1_bc[:], b1.rearrange("(a d) -> a d", a=1).broadcast_to([P, D])).then_inc(S["consts"], 16)
            sp.dma_start(eps_sb[:], eps.rearrange("(a d) -> a d", a=1).broadcast_to([P, 1])).then_inc(S["consts"], 16)
            sp.dma_start(row[0:B * T, 0, 0:P], nodemask.rearrange("b (t p) -> (b t) p", p=P)).then_inc(S["consts"], 16)

            def load_adjacency(b):
                for q in range(4):
                    sp.dma_start(a_rows[:, 2 * q:2 * q + 2, :], a_v[b, :, 2 * q:2 * q + 2, :]).then_inc(S[f"a_loaded{q}"], 16)

            def load_features(b):
                sp.dma_start(x_in[:], x_v[b]).then_inc(S["x_loaded"], 16)

            load_features(0)
            load_adjacency(0)

            def graph(b, more):
                if more:
                    sp.wait_ge(S["transposed"], b * 3 * T + 3 * T)
                    sp.wait_ge(S["deg_sum"], b * T + T)
                    load_adjacency(b + 1)
                    sp.wait_ge(S["y0_ok"], b * T + T)
                    load_features(b + 1)
                sp.wait_ge(S["at_hi_eps"], b * 2 + 1)
                sp.wait_ge(S["at_lo_eps"], b * 2 + 1)
                sp.dma_start(nbr25[b, 0], f32(at_hi[0:NODES, 0, :])).then_inc(S["nbr_out"], 16)
                sp.dma_start(nbr25[b, 1], f32(at_lo[0:NODES, 0, :])).then_inc(S["nbr_out"], 16)
                sp.wait_ge(S["head_ok"], b + 1)
                sp.dma_start(x2head[b], head[:]).then_inc(S["head_out"], 16)
                for half in range(2):
                    sp.wait_ge(S["x3_ok"], b * T + TH * (half + 1))
                    rows = slice(TH * half, TH * (half + 1))
                    sp.dma_start(x3_v[b, :, rows, :], xres[:, rows, :]).then_inc(S["x3_out"], 16)
                sp.wait_ge(S["mix_ok"], b * 4 + 4)
                sp.dma_start(mixed[b], mix_sb[:]).then_inc(S["mix_out"], 16)

            with sp.Fori(0, B - 1) as i:
                graph(i, True)
            graph(B - 1, False)
            sp.wait_ge(S["nbr_out"], 32 * B)
            sp.wait_ge(S["head_out"], 16 * B + 16)
            sp.wait_ge(S["x3_out"], 32 * B + 32)
            sp.wait_ge(S["mix_out"], 16 * B + 16)

        @block.tensor
        def _(pe):
            pe.wait_ge(S["consts"], 16 * 7)
            nc.tensor.transpose(tr[0][:, 0:B * T], row[0:B * T, 0, 0:P], ident[0:B * T, 0:B * T]).then_inc(S["setup_t"], 1)
            pe.wait_ge(S["setup_v"], 5)

            def transpose_a(b, k, half, after):
                if half == 1:
                    pe.wait_ge(S["at_lo_ok"], b * 2 * T + 2 * k + 1)
                elif after or k > 0:
                    pe.wait_ge(S["xt_lo_ok"], b * T + k)
                if k == 0:
                    for q in (2 * half, 2 * half + 1):
                        pe.wait_ge(S[f"a_loaded{q}"], b * 16 + 16)
                for j in range(4):
                    last = nc.tensor.transpose(tr[(3 * k + 2 * half) % 2][:, j * P:(j + 1) * P],
                                               a_rows[:, 4 * half + j, k * P:(k + 1) * P], ident[:])
                last.then_inc(S["transposed"], 1)

            def transpose_x(b, k, after):
                if after or k > 0:
                    pe.wait_ge(S["at_lo_ok"], b * 2 * T + 2 * k)
                if k == 0:
                    pe.wait_ge(S["x_loaded"], b * 16 + 16)
                for j in range(DT):
                    last = nc.tensor.transpose(tr[(3 * k + 1) % 2][:, j * P:(j + 1) * P],
                                               x_in[:, k, j * P:(j + 1) * P], ident[:])
                last.then_inc(S["transposed"], 1)

            def support0(b, k, after):
                pe.wait_ge(S["xt_hi_ok"], b * T + k + 1)
                pe.wait_ge(S["xt_lo_ok"], b * T + k + 1)
                if k >= 2:
                    pe.wait_ge(S["sup_ok"], b * T + k - 1)
                elif after:
                    pe.wait_ge(S["row1_ok"], b * T - 2 + k + 1)
                for j in range(DT):
                    last = split_matmuls(nc, nt[k % 2][:], xt_hi[:, k % 2, j, :], xt_lo[:, k % 2, j, :],
                                         w0_hi[:, j, :], w0_lo[:, j, :], j == 0, j == DT - 1)
                last.then_inc(S["sup_psum"], 1)

            def layer0(b):
                for n in range(T):
                    if n < 2:
                        pe.wait_ge(S["sup_ok"], b * T + T - 1 + n)
                    else:
                        pe.wait_ge(S["row0_ok"], b * T + n - 1)
                    for k in range(T):
                        if n == 0:
                            pe.wait_ge(S["mv_lo_ok"], b * T + k + 1)
                            pe.wait_ge(S["at_lo_ok"], b * 2 * T + 2 * k + 2)
                        cols = slice(n * P, (n + 1) * P)
                        last = split_matmuls(nc, nt[n % 2][:], at_hi[:, k, cols], at_lo[:, k, cols],
                                             mv0_hi[:, k * D:(k + 1) * D], mv0_lo[:, k * D:(k + 1) * D],
                                             k == 0, k == T - 1)
                    last.then_inc(S["m0_psum"], 1)

            def support1(b, n):
                if n % TH == 0:
                    pe.wait_ge(S["z_lo_ok"], b * 4 + 2 * (n // TH) + 2)
                if n < 2:
                    pe.wait_ge(S["row0_ok"], b * T + T - 1 + n)
                else:
                    pe.wait_ge(S["row1_ok"], b * T + n - 1)
                for j in range(DT):
                    cols = slice(j * N + n * P, j * N + (n + 1) * P)
                    nc.tensor.matmul(nt[n % 2][:], mv0_hi[:, cols], dw[:, j, :], start=j == 0, stop=False)
                    last = nc.tensor.matmul(nt[n % 2][:], mv0_lo[:, cols], dw[:, j, :], start=False, stop=j == DT - 1)
                last.then_inc(S["m1_psum"], 1)

            def layer1(b):
                for half in range(2):
                    for k in range(T):
                        if half == 0:
                            pe.wait_ge(S["x1_lo_ok"], b * T + k + 1)
                        for j in range(DT):
                            last = split_matmuls(nc, acc[2 * half + j][:],
                                                 x1_hi[:, k, j * P:(j + 1) * P], x1_lo[:, k, j * P:(j + 1) * P],
                                                 at_hi[:, k, half * H:(half + 1) * H], at_lo[:, k, half * H:(half + 1) * H],
                                                 k == 0, k == T - 1)
                            if k == T - 1:
                                last.then_inc(S["z_psum"], 1)
                        if half == 1 and 1 <= k <= TH:
                            support1(b, k - 1)

            def layer3_sum(b, k, half, j):
                if half == 0 and j == 0:
                    pe.wait_ge(S["x3_lo_ok"], b * T + k + 1)
                    if k % TH == 0:
                        pe.wait_ge(S["at_hi_eps"], b * 2 + k // TH + 1)
                        pe.wait_ge(S["at_lo_eps"], b * 2 + k // TH + 1)
                last = split_matmuls(nc, acc[2 * half + j][:],
                                     x3_hi[:, k, j * P:(j + 1) * P], x3_lo[:, k, j * P:(j + 1) * P],
                                     at_hi[:, k, half * H:(half + 1) * H], at_lo[:, k, half * H:(half + 1) * H],
                                     k == 0, k == T - 1)
                if k == T - 1:
                    last.then_inc(S["mix_psum"], 1)

            def layer3_and_prepare(b, more):
                for k in range(T):
                    layer3_sum(b, k, 0, 0)
                    layer3_sum(b, k, 0, 1)
                    if k == 0:
                        for n in range(TH, T):
                            support1(b, n)
                    if more:
                        transpose_a(b + 1, k, 0, True)
                    layer3_sum(b, k, 1, 0)
                    if more:
                        transpose_x(b + 1, k, True)
                    layer3_sum(b, k, 1, 1)
                    if more:
                        transpose_a(b + 1, k, 1, True)
                        if k > 0:
                            support0(b + 1, k - 1, True)
                if more:
                    support0(b + 1, T - 1, True)

            for k in range(T):
                transpose_a(0, k, 0, False)
                transpose_x(0, k, False)
                transpose_a(0, k, 1, False)
                if k > 0:
                    support0(0, k - 1, False)
            support0(0, T - 1, False)
            with pe.Fori(0, B - 1) as i:
                layer0(i)
                layer1(i)
                layer3_and_prepare(i, True)
            layer0(B - 1)
            layer1(B - 1)
            layer3_and_prepare(B - 1, False)

        @block.scalar
        def _(act):
            act.wait_ge(S["consts"], 16 * 7)
            nc.scalar.activation(w0_hi[:], w_stage[:, 0:DT, :], ACT.Copy).then_inc(S["setup_a"], 1)
            nc.scalar.activation(epsi[:], ident[:], ACT.Copy, scale=eps_sb[:, 0:1]).then_inc(S["setup_a"], 1)

            def row_sum(b, t, first=False):
                if t % 2 == 0:
                    act.wait_ge(S[f"a_loaded{t // 2}"], b * 16 + 16)
                if not first:
                    act.wait_ge(S["deg_sum"], b * T + t)
                nc.scalar.activation(junk[:], a_rows[:, t, :], ACT.Copy, accum_out=degs[:, t:t + 1])\
                    .then_inc(S["deg_sum"], 1)

            def prepare(b, k):
                if k < T:
                    for use, half in enumerate((0, None, 1)):
                        act.wait_ge(S["transposed"], b * 3 * T + 3 * k + use + 1)
                        bank = tr[(3 * k + use) % 2]
                        if half is not None:
                            nc.scalar.activation(at_hi[:, k, half * H:(half + 1) * H], bank[:], ACT.Copy)\
                                .then_inc(S["at_hi_ok"], 1)
                        else:
                            if k >= 2:
                                act.wait_ge(S["sup_psum"], b * T + k - 1)
                            nc.scalar.activation(xt_hi[:, k % 2], bank[:, 0:D].rearrange("p (j c) -> p j c", j=DT),
                                                 ACT.Copy).then_inc(S["xt_hi_ok"], 1)
                if 0 < k <= T:
                    if k == 1:
                        act.wait_ge(S["dism_ok"], b + 1)
                    act.wait_ge(S["sup_ok"], b * T + k)
                    nc.scalar.activation(mv0_hi[:, (k - 1) * D:k * D], sup[:, k - 1, :], ACT.Copy,
                                         scale=dis[:, k - 1:k]).then_inc(S["mv_hi_ok"], 1)

            def z_high(b, half):
                for j in range(DT):
                    act.wait_ge(S["z_psum"], b * 4 + 2 * half + j + 1)
                    nc.scalar.activation(mv0_hi[:, j * N + half * H:j * N + (half + 1) * H], acc[2 * half + j][:], ACT.Copy)\
                        .then_inc(S["z_hi_ok"], 1)

            def diag_high(b, half):
                act.wait_ge(S["diag_ok"], b * 4 + 4)
                for dst, tiles in diag_tiles(at_hi, half):
                    last = nc.scalar.activation(dst, diag[:, tiles, :], ACT.Copy)
                last.then_inc(S["at_hi_eps"], 1)

            def chain(b, s):
                n = s - 3
                if n == 0:
                    act.wait_ge(S["x2_ok"], b * T + 1)
                    act.wait_ge(S["head_out"], b * 16 + 16)
                    nc.scalar.activation(head[:], xres[0:NODES, 0, :], ACT.Copy).then_inc(S["head_ok"], 1)
                if 0 <= n < T:
                    act.wait_ge(S["x3_ok"], b * T + n + 1)
                    nc.scalar.activation(x3_hi[:, n, :], xres[:, n, :], ACT.Copy).then_inc(S["x3_hi_ok"], 1)

            def relu1(b, n):
                act.wait_ge(S["row1_ok"], b * T + n + 1)
                nc.scalar.activation(row[:, n % R, :], row[:, n % R, :], ACT.Relu).then_inc(S["relu1_ok"], 1)

            def graph(b, more):
                for s in range(T + 3):
                    if s < T:
                        act.wait_ge(S["row0_ok"], b * T + s + 1)
                        nc.scalar.activation(row[:, s % R, :], row[:, s % R, :], ACT.Relu, scale=dism[:, s:s + 1])\
                            .then_inc(S["relu0_ok"], 1)
                    n = s - 2
                    if 0 <= n < T:
                        act.wait_ge(S["x1_ok"], b * T + n + 1)
                        nc.scalar.activation(x1_hi[:, n, :], xres[:, n, :], ACT.Copy).then_inc(S["x1_hi_ok"], 1)
                if more:
                    for t in range(T // 2 + 1):
                        row_sum(b + 1, t)
                z_high(b, 0)
                diag_high(b, 0)
                for s in range(TH + 1):
                    if s < TH:
                        relu1(b, s)
                    chain(b, s)
                    if more and T // 2 + 1 + s < T:
                        row_sum(b + 1, T // 2 + 1 + s)
                z_high(b, 1)
                diag_high(b, 1)
                for n in range(TH, T):
                    relu1(b, n)
                for k in range(T + 1):
                    chain(b, TH + 1 + k)
                    if more:
                        if k == 0:
                            act.wait_ge(S["nbr_out"], b * 32 + 32)
                        prepare(b + 1, k)
                act.wait_ge(S["mix_out"], b * 16 + 16)
                for j in range(4):
                    act.wait_ge(S["mix_psum"], b * 4 + j + 1)
                    nc.scalar.activation(mix_sb[:, (j % 2) * 2 + j // 2, :], acc[j][:], ACT.Copy).then_inc(S["mix_ok"], 1)

            for t in range(T):
                row_sum(0, t, t == 0)
            for k in range(T + 1):
                prepare(0, k)
            with act.Fori(0, B - 1) as i:
                graph(i, True)
            graph(B - 1, False)

        @block.vector
        def _(dve):
            V = nc.vector
            dve.wait_ge(S["consts"], 16 * 7)
            dve.wait_ge(S["setup_a"], 1)
            V.tensor_tensor(w0_lo[:], w_stage[:, 0:DT, :], f32(w0_hi[:]), ALU.subtract).then_inc(S["setup_v"], 1)
            V.tensor_scalar(dw[:], w_stage[:, DT:2 * DT, :], -QUANT, None, ALU.is_lt).then_inc(S["setup_v"], 1)
            dve.wait_ge(S["setup_v"], 2)
            V.scalar_tensor_tensor(dw[:], w_stage[:, DT:2 * DT, :], QUANT, f32(dw[:]), ALU.is_gt, ALU.subtract)\
                .then_inc(S["setup_v"], 1)
            V.memset(minus_half[:], -0.5).then_inc(S["setup_v"], 1)
            dve.wait_ge(S["setup_t"], 1)
            V.tensor_copy(masks[:], tr[0][:, 0:B * T]).then_inc(S["setup_v"], 1)
            dve.wait_ge(S["setup_v"], 5)
            dve.wait_ge(S["setup_a"], 2)

            def degrees(b):
                dve.wait_ge(S["deg_sum"], b * T + T)
                V.tensor_scalar(degs[:], degs[:], 1.0, DEG_EPS, ALU.add, ALU.add).then_inc(S["deg_ok"], 1)

            def prepare(b, k):
                if k < T:
                    a_low(b, k, 0)
                if 1 < k <= T + 1:
                    n = k - 2
                    dve.wait_ge(S["mv_hi_ok"], b * T + n + 1)
                    V.scalar_tensor_tensor(mv0_lo[:, n * D:(n + 1) * D], sup[:, n, :], dis[:, n:n + 1],
                                           f32(mv0_hi[:, n * D:(n + 1) * D]), ALU.mult, ALU.subtract)\
                        .then_inc(S["mv_lo_ok"], 1)
                if k < T:
                    dve.wait_ge(S["xt_hi_ok"], b * T + k + 1)
                    V.tensor_tensor(xt_lo[:, k % 2], tr[(3 * k + 1) % 2][:, 0:D].rearrange("p (j c) -> p j c", j=DT),
                                    f32(xt_hi[:, k % 2]), ALU.subtract).then_inc(S["xt_lo_ok"], 1)
                    a_low(b, k, 1)
                if 0 < k <= T:
                    dve.wait_ge(S["sup_psum"], b * T + k)
                    V.tensor_tensor(sup[:, k - 1, :], nt[(k - 1) % 2][:], b0_bc[:], ALU.add).then_inc(S["sup_ok"], 1)

            def a_low(b, k, half):
                dve.wait_ge(S["at_hi_ok"], b * 2 * T + 2 * k + half + 1)
                cols = slice(half * H, (half + 1) * H)
                V.tensor_tensor(at_lo[:, k, cols], tr[(3 * k + 2 * half) % 2][:], f32(at_hi[:, k, cols]), ALU.subtract)\
                    .then_inc(S["at_lo_ok"], 1)

            def statistics(b, n, layer, y, a, c, var):
                if y:
                    dve.wait_ge(S[y], b * T + n + 1)
                V.bn_stats(stats[:, n % 4, :], xres[:, n, :]).then_inc(S[a], 1)
                dve.wait_ge(S[a], b * T + n + 1)
                V.memset(spacer[:], 0.0)
                V.bn_aggr(mean_var[:, layer, n, :], stats[:, n % 4, :]).then_inc(S[c], 1)
                dve.wait_ge(S[c], b * T + n + 1)
                V.tensor_scalar(var_eps[:, layer, n:n + 1], mean_var[:, layer, n, 1:2], LN_EPS, None, ALU.add)\
                    .then_inc(S[var], 1)

            def normalise(b, n, layer, powed, done):
                dve.wait_ge(S[powed], b * T + n + 1)
                V.tensor_scalar(xres[:, n, :], xres[:, n, :], mean_var[:, layer, n, 0:1], rstd[:, layer, n:n + 1],
                                ALU.subtract, ALU.mult).then_inc(S[done], 1)

            def z_low(b, half):
                for j in range(DT):
                    dve.wait_ge(S["z_hi_ok"], b * 4 + 2 * half + j + 1)
                    cols = slice(j * N + half * H, j * N + (half + 1) * H)
                    V.tensor_tensor(mv0_lo[:, cols], acc[2 * half + j][:], f32(mv0_hi[:, cols]), ALU.subtract)\
                        .then_inc(S["z_lo_ok"], 1)

            def diag_low(b, half):
                dve.wait_ge(S["at_hi_eps"], b * 2 + half + 1)
                for (dst, tiles), (hi, _) in zip(diag_tiles(at_lo, half), diag_tiles(at_hi, half)):
                    last = V.tensor_tensor(dst, diag[:, tiles, :], f32(hi), ALU.subtract)
                last.then_inc(S["at_lo_eps"], 1)

            def row1(b, n):
                dve.wait_ge(S["m1_psum"], b * T + n + 1)
                V.scalar_tensor_tensor(row[:, n % R, :], nt[n % 2][:], QUANT, b1_bc[:], ALU.mult, ALU.add)\
                    .then_inc(S["row1_ok"], 1)

            def chain(b, s):
                if 0 <= s - 1 < T:
                    statistics(b, s - 1, 1, "y1_ok", "st1_a", "st1_b", "var1_ok")
                if 0 <= s - 3 < T:
                    if s == 3:
                        dve.wait_ge(S["head_ok"], b + 1)
                    normalise(b, s - 3, 2, "pow2_ok", "x3_ok")
                if 0 <= s - 2 < T:
                    normalise(b, s - 2, 1, "pow1_ok", "x2_ok")
                    dve.wait_ge(S["x2_ok"], b * T + s - 1)
                    statistics(b, s - 2, 2, None, "st2_a", "st2_b", "var2_ok")

            def graph(b, more):
                for s in range(T + 3):
                    if s < T:
                        dve.wait_ge(S["m0_psum"], b * T + s + 1)
                        V.scalar_tensor_tensor(row[:, s % R, :], sup[:, s, :], dis[:, s:s + 1], nt[s % 2][:],
                                               ALU.mult, ALU.add).then_inc(S["row0_ok"], 1)
                    if 0 <= s - 2 < T:
                        normalise(b, s - 2, 0, "pow0_ok", "x1_ok")
                    if 0 <= s - 1 < T:
                        statistics(b, s - 1, 0, "y0_ok", "st0_a", "st0_b", "var0_ok")
                    if 0 <= s - 3 < T:
                        x1_low(b, s - 3)
                z_low(b, 0)
                diag_low(b, 0)
                for s in range(TH + 1):
                    if s < TH:
                        row1(b, s)
                    chain(b, s)
                z_low(b, 1)
                diag_low(b, 1)
                for n in range(TH, T):
                    row1(b, n)
                if more:
                    degrees(b + 1)
                for k in range(T + 2):
                    chain(b, TH + 1 + k)
                    if more:
                        prepare(b + 1, k)

            def x1_low(b, n):
                dve.wait_ge(S["x1_hi_ok"], b * T + n + 1)
                V.tensor_tensor(x1_lo[:, n, :], xres[:, n, :], f32(x1_hi[:, n, :]), ALU.subtract)\
                    .then_inc(S["x1_lo_ok"], 1)

            degrees(0)
            for k in range(T + 2):
                prepare(0, k)
            with dve.Fori(0, B - 1) as i:
                graph(i, True)
            graph(B - 1, False)

        @block.gpsimd
        def _(pool):
            G = nc.gpsimd
            pool.sem_inc(S["head_out"], 16)
            pool.sem_inc(S["mix_out"], 16)
            pool.sem_inc(S["x3_out"], 32)
            pool.wait_ge(S["setup_v"], 5)
            pool.wait_ge(S["setup_a"], 2)

            def inverse_roots(b):
                pool.wait_ge(S["deg_ok"], b + 1)
                G.tensor_tensor(dis[:], degs[:], minus_half[:], ALU.pow).then_inc(S["dis_pow"], 1)
                pool.wait_ge(S["dis_pow"], b + 1)
                G.tensor_tensor(dism[:], dis[:], masks[:, bass.ds(b * T, T)], ALU.mult).then_inc(S["dism_ok"], 1)

            def power(b, n, layer, var, done):
                pool.wait_ge(S[var], b * T + n + 1)
                G.tensor_tensor(rstd[:, layer, n:n + 1], var_eps[:, layer, n:n + 1], minus_half[:, 0:1], ALU.pow)\
                    .then_inc(S[done], 1)

            def diagonal(b, half):
                his, los = diag_tiles(at_hi, half), diag_tiles(at_lo, half)
                for (hi, tiles), (lo, _) in zip(his, los):
                    last = G.tensor_tensor(diag[:, tiles, :], f32(hi), f32(lo), ALU.add)
                last.then_inc(S["diag_ok"], 1)
                pool.wait_ge(S["diag_ok"], b * 4 + 2 * half + 1)
                rows = slice(TH * half, TH * (half + 1))
                G.tensor_tensor(diag[:, rows, :], diag[:, rows, :], epsi[:].unsqueeze(1).broadcast_to([P, TH, P]),
                                ALU.add).then_inc(S["diag_ok"], 1)

            def residual1(b, n):
                pool.wait_ge(S["relu1_ok"], b * T + n + 1)
                G.tensor_tensor(xres[:, n, :], row[:, n % R, :], xres[:, n, :], ALU.add).then_inc(S["y1_ok"], 1)

            def chain(b, s):
                if 0 <= s - 1 < T:
                    power(b, s - 1, 1, "var1_ok", "pow1_ok")
                if 0 <= s - 2 < T:
                    power(b, s - 2, 2, "var2_ok", "pow2_ok")
                if 0 <= s - 3 < T:
                    n = s - 3
                    pool.wait_ge(S["x3_hi_ok"], b * T + n + 1)
                    last = G.tensor_tensor(x3_lo[:, n, :], xres[:, n, :], f32(x3_hi[:, n, :]), ALU.subtract)
                    if n > 0:
                        last.then_inc(S["x3_lo_ok"], 1)
                    else:
                        last.then_inc(S["x3_lo0"], 1)
                        pool.wait_ge(S["x3_lo0"], b + 1)
                        G.tensor_tensor(spacer_p[:], minus_half[:, 0:1], minus_half[:, 0:1], ALU.add)
                        G.memset(f32(x3_hi[0:NODES, 0, :]), 0.0)
                        G.memset(f32(x3_lo[0:NODES, 0, :]), 0.0).then_inc(S["x3_lo_ok"], 1)

            def graph(b, more):
                pool.wait_ge(S["x3_out"], b * 32 + 32)
                for s in range(T + 1):
                    if s < T:
                        pool.wait_ge(S["relu0_ok"], b * T + s + 1)
                        G.tensor_tensor(xres[:, s, :], row[:, s % R, :], x_in[:, s, :], ALU.add).then_inc(S["y0_ok"], 1)
                    if s > 0:
                        power(b, s - 1, 0, "var0_ok", "pow0_ok")
                    if s in (2, 4):
                        diagonal(b, s // 2 - 1)
                for s in range(TH + 1):
                    if s < TH:
                        residual1(b, s)
                    chain(b, s)
                for n in range(TH, T):
                    residual1(b, n)
                if more:
                    inverse_roots(b + 1)
                for s in range(TH + 1, T + 3):
                    chain(b, s)

            inverse_roots(0)
            with pool.Fori(0, B - 1) as i:
                graph(i, True)
            graph(B - 1, False)


def group_tiles(B):
    tiles = []
    for g, per in enumerate((4, 8, 16, 16, 16)):
        per = min(per, B)
        tiles += [(g, b0, per) for b0 in range(0, B, per)]
    return tiles


def runs(nodes):
    out = []
    for i, n in enumerate(nodes):
        if out and out[-1][1] + out[-1][2] == n:
            out[-1][2] += 1
        else:
            out.append([i, n, 1])
    return out


def scatters(B):
    tiles = group_tiles(B)
    return [(t, u) for u, (h, c0, nc0) in enumerate(tiles) if h == 0
            for t, (g, b0, nb) in enumerate(tiles) if g > 0 and b0 <= c0 < b0 + nb]


def layout_constants(B):
    tiles = group_tiles(B)
    same = np.zeros((P, len(tiles), 16), np.float32)
    for t, (g, b0, nb) in enumerate(tiles):
        for r in range(len(GROUPS[g]) * nb):
            same[r, t, r % nb] = 1
    pairs = scatters(B)
    place = np.zeros((P, len(pairs), P), np.float32)
    for q, (t, u) in enumerate(pairs):
        (g, b0, nb), (_, c0, nc0) = tiles[t], tiles[u]
        for i, node in enumerate(GROUPS[g]):
            for c in range(nc0):
                place[i * nb + c0 + c - b0, q, node * nc0 + c] = 1
    return np.eye(P, dtype=np.float32), same, place


def part2(nc, adj, x2head, w1, b1, w2, b2, fusion, eye, same, place, x3, headsplit):
    B = adj.shape[0]
    G5, D, HID = w1.shape
    DT, HT = D // P, HID // P
    tiles = group_tiles(B)
    NT = len(tiles)
    rows = [len(GROUPS[g]) * nb for g, _, nb in tiles]
    NU = sum(g == 0 for g, _, _ in tiles)
    pairs = scatters(B)
    assert max(rows) <= P

    with ExitStack() as ctx:
        def sb(name, shape, dt=F32):
            return ctx.enter_context(nc.sbuf_tensor(name, shape, dt))

        def ps(name):
            return ctx.enter_context(nc.psum_tensor(name, [P, 512], F32))

        w1_hi, w1_lo = sb("w1_hi", [P, G5, DT * HID], F32R), sb("w1_lo", [P, G5, DT * HID], F32R)
        w2_hi, w2_lo = sb("w2_hi", [P, G5, HT * D], F32R), sb("w2_lo", [P, G5, HT * D], F32R)
        raw = sb("raw", [P, 4, DT * HID])
        b1_bc, b2_bc = sb("g_b1", [P, G5, HID]), sb("g_b2", [P, G5, D])
        xg = sb("xg", [P, NT, D])
        cadj = sb("cadj", [P, NT, NODES])
        bd = sb("bd", [P, NT, P])
        bt_hi, bt_lo = sb("bt_hi", [P, NT, P], F32R), sb("bt_lo", [P, NT, P], F32R)
        xt_hi, xt_lo = sb("g_xt_hi", [P, 2, DT, P], F32R), sb("g_xt_lo", [P, 2, DT, P], F32R)
        s1_hi, s1_lo = sb("s1_hi", [P, 2, HID], F32R), sb("s1_lo", [P, 2, HID], F32R)
        hid = sb("hid", [P, 2, HID])
        ht_hi, ht_lo = sb("ht_hi", [P, 2, HT, P], F32R), sb("ht_lo", [P, 2, HT, P], F32R)
        s2_hi, s2_lo = sb("s2_hi", [P, 2, D], F32R), sb("s2_lo", [P, 2, D], F32R)
        og = sb("og", [P, NT, D])
        xn_hi, xn_lo = sb("xn_hi", [P, NU, D], F32R), sb("xn_lo", [P, NU, D], F32R)
        ident, same_sb, place_sb = sb("g_id", [P, P]), sb("same_sb", [P, NT, 16]), sb("place_sb", [P, len(pairs), P])
        deg, nonzero, dinv = sb("g_deg", [P, NT]), sb("g_nz", [P, NT]), sb("g_dinv", [P, NT])
        half = sb("g_half", [P, NT])
        fw, fmax, fsum = sb("fw", [P, G5]), sb("fmax", [P, 1]), sb("fsum", [P, 1])
        stats, mean_var = sb("g_stats", [P, NU, 6]), sb("g_mv", [P, NU, 2])
        var_eps, rstd = sb("g_ve", [P, NU]), sb("g_rstd", [P, NU])

        p_a, p_b, p_c, p_d, p_e, p_f = (ps(f"g_psum_{c}") for c in "abcdef")
        p_u = [ps(f"g_psum_u{i}") for i in range(2)]

        names = ["small_in", "w_in0", "w_in1", "w_in2", "w_in3", "w_hi_ok", "w_lo_ok", "prep", "bd_a", "bd_b", "bd_ok",
                 "deg_ok", "dinv_a", "dinv_ok", "fuse", "half_ok",
                 "a_psum", "a_hi_ok", "a_lo_ok", "b_psum", "b_hi_ok", "b_lo_ok", "c_psum", "c_ok", "c_relu",
                 "d_psum", "d_hi_ok", "d_lo_ok", "e_psum", "e_hi_ok", "e_lo_ok", "f_psum", "f_ok", "f_relu",
                 "u_psum", "u_a", "u_y", "u_st", "u_mv", "u_ve", "u_pow", "u_x", "u_hi", "u_lo", "stored"]
        S = {n: ctx.enter_context(nc.semaphore("p2_" + n)) for n in names}
        n_small = [0]

        block = ctx.enter_context(nc.Block("part2"))
        small_loads = 6 + sum(len(runs(GROUPS[g])) + len(runs(GROUPS[g])) ** 2 for g, _, _ in tiles)

        @block.sync
        def _(sp):
            def small(dst, src):
                sp.dma_start(dst, src, allow_slow_non_contiguous=True).then_inc(S["small_in"], 16)
                n_small[0] += 1

            small(ident[:], eye)
            small(same_sb[:], same)
            small(place_sb[:], place)
            small(b1_bc[:], b1.unsqueeze(0).broadcast_to([P, G5, HID]))
            small(b2_bc[:], b2.unsqueeze(0).broadcast_to([P, G5, D]))
            small(fw[:], fusion.unsqueeze(0).broadcast_to([P, G5]))
            for t, (g, b0, nb) in enumerate(tiles):
                for i, n, k in runs(GROUPS[g]):
                    part = slice(i * nb, (i + k) * nb)
                    small(xg[part, t, :], x2head[b0:b0 + nb, n:n + k, :].rearrange("b i d -> i b d"))
                    for j, m, kk in runs(GROUPS[g]):
                        small(cadj[part, t, j:j + kk], adj[b0:b0 + nb, n:n + k, m:m + kk].rearrange("b i m -> i b m"))
            assert n_small[0] == small_loads, n_small

            for q in range(2 * G5):
                if q >= 4:
                    sp.wait_ge(S["w_lo_ok"], q - 3)
                src = (w1, w2)[q % 2][q // 2].rearrange("(k p) o -> p k o", p=P)
                sp.dma_start(raw[:, q % 4, :].rearrange("p (k o) -> p k o", k=(DT, HT)[q % 2]), src)\
                    .then_inc(S[f"w_in{q % 4}"], 16)
            for u in range(NU):
                _, b0, nb = tiles[u]
                r = rows[u]
                sp.wait_ge(S["u_x"], u + 1)
                sp.dma_start(x3[b0:b0 + nb, 0:NODES, :].rearrange("b i d -> i b d"), xg[0:r, u, :]).then_inc(S["stored"], 16)
                sp.wait_ge(S["u_lo"], u + 1)
                sp.dma_start(headsplit[b0:b0 + nb, 0].rearrange("b i d -> i b d"), f32(xn_hi[0:r, u, :])).then_inc(S["stored"], 16)
                sp.dma_start(headsplit[b0:b0 + nb, 1].rearrange("b i d -> i b d"), f32(xn_lo[0:r, u, :])).then_inc(S["stored"], 16)
            sp.wait_ge(S["stored"], 48 * NU)

        @block.tensor
        def _(pe):
            T_ = nc.tensor

            def stage_a(t):
                r = rows[t]
                pe.wait_ge(S["bd_ok"], t + 1)
                if t > 0:
                    pe.wait_ge(S["a_lo_ok"], 2 * t)
                for j in range(DT):
                    T_.transpose(p_a[:, j * P:j * P + r], xg[0:r, t, j * P:(j + 1) * P], ident[0:r, 0:r])
                T_.transpose(p_a[0:r, DT * P:DT * P + r], bd[0:r, t, 0:r], ident[0:r, 0:r]).then_inc(S["a_psum"], 1)

            def stage_b(t):
                g, r = tiles[t][0], rows[t]
                pe.wait_ge(S["w_lo_ok"], 2 * g + 1)
                pe.wait_ge(S["a_lo_ok"], 2 * t + 2)
                if t > 0:
                    pe.wait_ge(S["b_lo_ok"], t)
                for j in range(DT):
                    last = split_matmuls(nc, p_b[0:r, :], xt_hi[:, t % 2, j, 0:r], xt_lo[:, t % 2, j, 0:r],
                                         w1_hi[:, g, j * HID:(j + 1) * HID], w1_lo[:, g, j * HID:(j + 1) * HID],
                                         j == 0, j == DT - 1)
                last.then_inc(S["b_psum"], 1)

            def stage_c(t):
                r = rows[t]
                pe.wait_ge(S["b_lo_ok"], t + 1)
                if t > 0:
                    pe.wait_ge(S["c_ok"], t)
                split_matmuls(nc, p_c[0:r, :], bt_hi[0:r, t, 0:r], bt_lo[0:r, t, 0:r], s1_hi[0:r, t % 2, :],
                              s1_lo[0:r, t % 2, :], True, True).then_inc(S["c_psum"], 1)

            def stage_d(t):
                r = rows[t]
                pe.wait_ge(S["c_relu"], t + 1)
                if t > 0:
                    pe.wait_ge(S["d_lo_ok"], t)
                for j in range(HT):
                    last = T_.transpose(p_d[:, j * P:j * P + r], hid[0:r, t % 2, j * P:(j + 1) * P], ident[0:r, 0:r])
                last.then_inc(S["d_psum"], 1)

            def stage_e(t):
                g, r = tiles[t][0], rows[t]
                pe.wait_ge(S["w_lo_ok"], 2 * g + 2)
                pe.wait_ge(S["d_lo_ok"], t + 1)
                if t > 0:
                    pe.wait_ge(S["e_lo_ok"], t)
                for j in range(HT):
                    last = split_matmuls(nc, p_e[0:r, 0:D], ht_hi[:, t % 2, j, 0:r], ht_lo[:, t % 2, j, 0:r],
                                         w2_hi[:, g, j * D:(j + 1) * D], w2_lo[:, g, j * D:(j + 1) * D],
                                         j == 0, j == HT - 1)
                last.then_inc(S["e_psum"], 1)

            def stage_f(t):
                r = rows[t]
                pe.wait_ge(S["e_lo_ok"], t + 1)
                if t > 0:
                    pe.wait_ge(S["f_ok"], t)
                split_matmuls(nc, p_f[0:r, 0:D], bt_hi[0:r, t, 0:r], bt_lo[0:r, t, 0:r], s2_hi[0:r, t % 2, :],
                              s2_lo[0:r, t % 2, :], True, True).then_inc(S["f_psum"], 1)

            for s in range(NT + 5):
                for lag, stage in ((5, stage_f), (4, stage_e), (3, stage_d), (2, stage_c), (1, stage_b), (0, stage_a)):
                    if 0 <= s - lag < NT:
                        stage(s - lag)
            pe.wait_ge(S["f_relu"], NT)
            for u in range(NU):
                if u >= 2:
                    pe.wait_ge(S["u_a"], u - 1)
                mine = [q for q, (_, v) in enumerate(pairs) if v == u]
                for n, q in enumerate(mine):
                    t = pairs[q][0]
                    last = T_.matmul(p_u[u % 2][0:rows[u], 0:D], place_sb[0:rows[t], q, 0:rows[u]], og[0:rows[t], t, :],
                                     start=n == 0, stop=n == len(mine) - 1)
                last.then_inc(S["u_psum"], 1)

        @block.scalar
        def _(act):
            A = nc.scalar.activation
            act.wait_ge(S["small_in"], 16 * small_loads)
            act.wait_ge(S["fuse"], 1)
            A(fw[:], fw[:], ACT.Exp, bias=fmax[:, 0:1], accum_out=fsum[:, 0:1]).then_inc(S["fuse"], 1)
            for q in range(2 * G5):
                act.wait_ge(S[f"w_in{q % 4}"], 16 * (q // 4 + 1))
                A((w1_hi, w2_hi)[q % 2][:, q // 2, :], raw[:, q % 4, :], ACT.Copy).then_inc(S["w_hi_ok"], 1)
            act.wait_ge(S["fuse"], 4)
            act.wait_ge(S["dinv_ok"], 1)

            def stage_a(t):
                r = rows[t]
                act.wait_ge(S["a_psum"], t + 1)
                A(xt_hi[:, t % 2, :, 0:r], p_a[:, 0:DT * P].rearrange("p (j c) -> p j c", j=DT)[:, :, 0:r], ACT.Copy)\
                    .then_inc(S["a_hi_ok"], 1)
                A(bt_hi[0:r, t, 0:r], p_a[0:r, DT * P:DT * P + r], ACT.Copy).then_inc(S["a_hi_ok"], 1)

            def stage_b(t):
                r = rows[t]
                act.wait_ge(S["b_psum"], t + 1)
                A(s1_hi[0:r, t % 2, :], p_b[0:r, :], ACT.Copy, scale=dinv[0:r, t:t + 1]).then_inc(S["b_hi_ok"], 1)

            def stage_c(t):
                r = rows[t]
                act.wait_ge(S["c_ok"], t + 1)
                A(hid[0:r, t % 2, :], hid[0:r, t % 2, :], ACT.Relu).then_inc(S["c_relu"], 1)

            def stage_d(t):
                r = rows[t]
                act.wait_ge(S["d_psum"], t + 1)
                A(ht_hi[:, t % 2, :, 0:r], p_d[:].rearrange("p (j c) -> p j c", j=HT)[:, :, 0:r], ACT.Copy)\
                    .then_inc(S["d_hi_ok"], 1)

            def stage_e(t):
                r = rows[t]
                act.wait_ge(S["e_psum"], t + 1)
                A(s2_hi[0:r, t % 2, :], p_e[0:r, 0:D], ACT.Copy, scale=dinv[0:r, t:t + 1]).then_inc(S["e_hi_ok"], 1)

            def stage_f(t):
                g, r = tiles[t][0], rows[t]
                act.wait_ge(S["f_ok"], t + 1)
                A(og[0:r, t, :], og[0:r, t, :], ACT.Relu, scale=fw[0:r, g:g + 1]).then_inc(S["f_relu"], 1)

            for s in range(NT + 5):
                for lag, stage in ((5, stage_f), (4, stage_e), (3, stage_d), (2, stage_c), (1, stage_b), (0, stage_a)):
                    if 0 <= s - lag < NT:
                        stage(s - lag)
            for u in range(NU):
                r = rows[u]
                act.wait_ge(S["u_x"], u + 1)
                A(xn_hi[0:r, u, :], xg[0:r, u, :], ACT.Copy).then_inc(S["u_hi"], 1)

        @block.vector
        def _(dve):
            V = nc.vector
            dve.wait_ge(S["small_in"], 16 * small_loads)
            V.memset(half[:], -0.5).then_inc(S["half_ok"], 1)
            V.memset(deg[:], 1.0).then_inc(S["prep"], 1)
            V.tensor_reduce(fmax[:], fw[:], mybir.AxisListType.X, ALU.max, negate=True).then_inc(S["fuse"], 1)
            dve.wait_ge(S["fuse"], 2)
            V.reciprocal(fsum[:], fsum[:]).then_inc(S["fuse"], 1)
            dve.wait_ge(S["fuse"], 3)
            V.tensor_scalar(fw[:], fw[:], fsum[:, 0:1], None, ALU.mult).then_inc(S["fuse"], 1)
            dve.wait_ge(S["prep"], 1)
            for t, (g, b0, nb) in enumerate(tiles):
                n, r = len(GROUPS[g]), rows[t]
                V.tensor_tensor(bd[0:r, t, 0:r].rearrange("p (j b) -> p j b", b=nb),
                                cadj[0:r, t, 0:n].unsqueeze(2).broadcast_to([r, n, nb]),
                                same_sb[0:r, t, 0:nb].unsqueeze(1).broadcast_to([r, n, nb]), ALU.mult)\
                    .then_inc(S["bd_a"], 1)
            for t in range(NT):
                r = rows[t]
                dve.wait_ge(S["bd_a"], t + 1)
                V.tensor_tensor(bd[0:r, t, 0:r], bd[0:r, t, 0:r], ident[0:r, 0:r], ALU.add).then_inc(S["bd_ok"], 1)
            for t in range(NT):
                r = rows[t]
                dve.wait_ge(S["bd_ok"], t + 1)
                V.tensor_reduce(deg[0:r, t:t + 1], bd[0:r, t, 0:r], mybir.AxisListType.X, ALU.add).then_inc(S["bd_b"], 1)
            dve.wait_ge(S["bd_b"], NT)
            V.tensor_scalar(nonzero[:], deg[:], 0.0, None, ALU.not_equal).then_inc(S["deg_ok"], 1)
            V.scalar_tensor_tensor(dinv[:], deg[:], 0.0, deg[:], ALU.is_equal, ALU.add).then_inc(S["deg_ok"], 1)

            def split_weights(q):
                dve.wait_ge(S["w_hi_ok"], q + 1)
                lo, hi = ((w1_lo, w1_hi), (w2_lo, w2_hi))[q % 2]
                V.tensor_tensor(lo[:, q // 2, :], raw[:, q % 4, :], f32(hi[:, q // 2, :]), ALU.subtract)\
                    .then_inc(S["w_lo_ok"], 1)

            for q in range(2 * G5):
                split_weights(q)
            dve.wait_ge(S["dinv_ok"], 1)

            def stage_a(t):
                r = rows[t]
                dve.wait_ge(S["a_hi_ok"], 2 * t + 2)
                V.tensor_tensor(xt_lo[:, t % 2, :, 0:r], p_a[:, 0:DT * P].rearrange("p (j c) -> p j c", j=DT)[:, :, 0:r],
                                f32(xt_hi[:, t % 2, :, 0:r]), ALU.subtract).then_inc(S["a_lo_ok"], 1)
                V.tensor_tensor(bt_lo[0:r, t, 0:r], p_a[0:r, DT * P:DT * P + r], f32(bt_hi[0:r, t, 0:r]), ALU.subtract)\
                    .then_inc(S["a_lo_ok"], 1)

            def stage_b(t):
                r = rows[t]
                dve.wait_ge(S["b_hi_ok"], t + 1)
                V.scalar_tensor_tensor(s1_lo[0:r, t % 2, :], p_b[0:r, :], dinv[0:r, t:t + 1], f32(s1_hi[0:r, t % 2, :]),
                                       ALU.mult, ALU.subtract).then_inc(S["b_lo_ok"], 1)

            def stage_c(t):
                g, r = tiles[t][0], rows[t]
                dve.wait_ge(S["c_psum"], t + 1)
                V.scalar_tensor_tensor(hid[0:r, t % 2, :], p_c[0:r, :], dinv[0:r, t:t + 1], b1_bc[0:r, g, :],
                                       ALU.mult, ALU.add).then_inc(S["c_ok"], 1)

            def stage_d(t):
                r = rows[t]
                dve.wait_ge(S["d_hi_ok"], t + 1)
                V.tensor_tensor(ht_lo[:, t % 2, :, 0:r], p_d[:].rearrange("p (j c) -> p j c", j=HT)[:, :, 0:r],
                                f32(ht_hi[:, t % 2, :, 0:r]), ALU.subtract).then_inc(S["d_lo_ok"], 1)

            def stage_e(t):
                r = rows[t]
                dve.wait_ge(S["e_hi_ok"], t + 1)
                V.scalar_tensor_tensor(s2_lo[0:r, t % 2, :], p_e[0:r, 0:D], dinv[0:r, t:t + 1], f32(s2_hi[0:r, t % 2, :]),
                                       ALU.mult, ALU.subtract).then_inc(S["e_lo_ok"], 1)

            def stage_f(t):
                g, r = tiles[t][0], rows[t]
                dve.wait_ge(S["f_psum"], t + 1)
                V.scalar_tensor_tensor(og[0:r, t, :], p_f[0:r, 0:D], dinv[0:r, t:t + 1], b2_bc[0:r, g, :],
                                       ALU.mult, ALU.add).then_inc(S["f_ok"], 1)

            for s in range(NT + 5):
                for lag, stage in ((5, stage_f), (4, stage_e), (3, stage_d), (2, stage_c), (1, stage_b), (0, stage_a)):
                    if 0 <= s - lag < NT:
                        stage(s - lag)
            for u in range(NU):
                r = rows[u]
                dve.wait_ge(S["u_psum"], u + 1)
                dve.wait_ge(S["f_relu"], NT)
                V.tensor_tensor(og[0:r, u, :], p_u[u % 2][0:r, 0:D], og[0:r, u, :], ALU.add).then_inc(S["u_a"], 1)
                dve.wait_ge(S["u_a"], u + 1)
                V.tensor_tensor(xg[0:r, u, :], xg[0:r, u, :], og[0:r, u, :], ALU.add).then_inc(S["u_y"], 1)
            for u in range(NU):
                r = rows[u]
                dve.wait_ge(S["u_y"], u + 1)
                V.bn_stats(stats[0:r, u, :], xg[0:r, u, :]).then_inc(S["u_st"], 1)
            for u in range(NU):
                r = rows[u]
                dve.wait_ge(S["u_st"], u + 1)
                V.bn_aggr(mean_var[0:r, u, :], stats[0:r, u, :]).then_inc(S["u_mv"], 1)
            for u in range(NU):
                r = rows[u]
                dve.wait_ge(S["u_mv"], u + 1)
                V.tensor_scalar(var_eps[0:r, u:u + 1], mean_var[0:r, u, 1:2], LN_EPS, None, ALU.add).then_inc(S["u_ve"], 1)
            for u in range(NU):
                r = rows[u]
                dve.wait_ge(S["u_pow"], u + 1)
                V.tensor_scalar(xg[0:r, u, :], xg[0:r, u, :], mean_var[0:r, u, 0:1], rstd[0:r, u:u + 1],
                                ALU.subtract, ALU.mult).then_inc(S["u_x"], 1)
            for u in range(NU):
                r = rows[u]
                dve.wait_ge(S["u_hi"], u + 1)
                V.tensor_tensor(xn_lo[0:r, u, :], xg[0:r, u, :], f32(xn_hi[0:r, u, :]), ALU.subtract).then_inc(S["u_lo"], 1)

        @block.gpsimd
        def _(pool):
            G = nc.gpsimd
            pool.wait_ge(S["half_ok"], 1)
            pool.wait_ge(S["deg_ok"], 2)
            G.tensor_tensor(dinv[:], dinv[:], half[:], ALU.pow).then_inc(S["dinv_a"], 1)
            pool.wait_ge(S["dinv_a"], 1)
            G.tensor_tensor(dinv[:], dinv[:], nonzero[:], ALU.mult).then_inc(S["dinv_ok"], 1)
            for u in range(NU):
                r = rows[u]
                pool.wait_ge(S["u_ve"], u + 1)
                G.tensor_tensor(rstd[0:r, u:u + 1], var_eps[0:r, u:u + 1], half[0:r, 0:1], ALU.pow).then_inc(S["u_pow"], 1)


def part3(nc, mixed, x3, nbr25, headsplit, v1, c1, rms_w, v2, c2, eye, out):
    B, N, D = x3.shape
    HID = v1.shape[1]
    H = N // 2
    DT, KT, RT = D // P, HID // P, H // P
    NB4 = 4 * NODES
    LAG = 5
    SR = 4
    U = 2 * B

    with ExitStack() as ctx:
        def sb(name, shape, dt=F32):
            return ctx.enter_context(nc.sbuf_tensor(name, shape, dt))

        def ps(name):
            return ctx.enter_context(nc.psum_tensor(name, [P, 512], F32))

        v1_hi, v1_lo = sb("v1_hi", [P, DT, HID], F32R), sb("v1_lo", [P, DT, HID], F32R)
        v2_hi, v2_lo = sb("v2_hi", [P, KT, D], F32R), sb("v2_lo", [P, KT, D], F32R)
        mix = sb("mix", [P, 2, DT, H])
        agg_hi, agg_lo = sb("agg_hi", [P, 2, DT, H], F32R), sb("agg_lo", [P, 2, DT, H], F32R)
        nbr, xnbr = sb("nbr", [NB4, N], F32R), sb("xnbr", [NB4, D], F32R)
        hb = sb("hb", [P, 2, KT, H])
        sq = sb("sq", [P, SR, H])
        ssum = sb("ssum", [P, 2, H])
        s_hi, s_lo = sb("s_hi", [P, SR, H], F32R), sb("s_lo", [P, SR, H], F32R)
        rdiag = sb("rdiag", [P, RT, P])
        xr = sb("xr", [P, 2, RT, D])
        ident, ones = sb("t_id", [P, P]), sb("t_ones", [P, P])
        cw_rows = sb("cw_rows", [2 * KT, P])
        cw = sb("cw", [P, 2 * KT])
        c2_bc = sb("c2_bc", [P, 2, D])
        ms, rr = sb("ms", [P, RT]), sb("rr", [P, RT])
        half, spacer = sb("t_half", [P, RT]), sb("t_spacer", [P, 1])
        stats, mean_var = sb("t_stats", [P, RT, 6]), sb("t_mv", [P, RT, 2])
        var_eps, rstd = sb("t_ve", [P, RT]), sb("t_rstd", [P, RT])
        raw = hb[:].rearrange("p a k n -> p (a k n)")

        hp = [ps(f"hp{i}") for i in range(2)]
        op = [[ps(f"op{i}{j}") for j in range(2)] for i in range(2)]
        cp, rb = ps("cp"), ps("rb")

        names = ["const_in", "setup_a", "setup_v", "setup_t", "mix_in0", "mix_in1", "nbr_in", "xr_in0", "xr_in1",
                 "corr_psum", "agg_ok", "agg_hi_ok", "agg_lo_ok", "hid_psum", "hb_ok", "sq_ok", "ss_ok",
                 "sum_psum", "ms_ok", "rr_ok", "rd_ok", "rb_psum", "t_ok", "silu_ok", "s_hi_ok", "s_lo_ok",
                 "o_step", "xb_ok", "y_ok", "st_ok", "mv_ok", "ve_ok", "pw_ok", "out_ok", "stored0", "stored1"]
        S = {n: ctx.enter_context(nc.semaphore("p3_" + n)) for n in names}
        block = ctx.enter_context(nc.Block("part3"))

        mix_v = mixed.rearrange("b p (j h) n -> b p h j n", h=2)
        x_v = x3.rearrange("b (h t p) d -> b h p t d", h=2, p=P)
        o_v = out.rearrange("b (h t p) d -> b h p t d", h=2, p=P)

        def back(unit, n):
            b, h = unit
            return (b - n // 2, h) if n % 2 == 0 else (b - (n + 1) // 2 + h, 1 - h)

        def upto(unit, per, count):
            b, h = unit
            return b * (2 * per) + (h * per + count)

        def wait(eng, name, value):
            if not isinstance(value, int) or value > 0:
                eng.wait_ge(S[name], value)

        def walk(eng, step):
            def units(b, cur=True, prev=((True, True), (True, True)), nxt=(True, True)):
                for h in range(2):
                    for j in range(KT):
                        step((b, h), j, cur, prev[h], nxt[h])

            units(0, prev=((False, False), (True, False)))
            with eng.Fori(1, B - 1) as b:
                units(b)
            units(B - 1, nxt=(True, False))
            units(B, cur=False, prev=((True, True), (False, True)), nxt=(False, False))

        def lagging(unit, j, lag, prev):
            n, k = (1, j - lag) if j >= lag else (2, j - lag + KT)
            return (back(unit, n), k) if prev[n - 1] else None

        @block.sync
        def _(sp):
            sp.dma_start(ident[:], eye).then_inc(S["const_in"], 16)
            sp.dma_start(raw[:, 0:DT * HID].rearrange("p (k n) -> p k n", k=DT), v1.rearrange("(k p) n -> p k n", p=P))\
                .then_inc(S["const_in"], 16)
            sp.dma_start(raw[:, DT * HID:DT * HID + KT * D].rearrange("p (k n) -> p k n", k=KT),
                         v2.rearrange("(k p) n -> p k n", p=P)).then_inc(S["const_in"], 16)
            sp.dma_start(cw_rows[0:KT, :], c1.rearrange("(k p) -> k p", p=P)).then_inc(S["const_in"], 16)
            sp.dma_start(cw_rows[KT:2 * KT, :], rms_w.rearrange("(k p) -> k p", p=P)).then_inc(S["const_in"], 16)
            for i in range(2):
                sp.dma_start(c2_bc[:, i, :], c2.rearrange("(a d) -> a d", a=1).broadcast_to([P, D])).then_inc(S["const_in"], 16)

            def load_mix(b, h):
                sp.dma_start(mix[:, h], mix_v[b, :, h]).then_inc(S[f"mix_in{h}"], 16)

            def load_neighbours(b):
                for i, (a, x_) in enumerate(((0, 0), (0, 1), (1, 0), (1, 1))):
                    part = slice(NODES * i, NODES * (i + 1))
                    sp.dma_start(f32(nbr[part, :]), nbr25[b, a]).then_inc(S["nbr_in"], 16)
                    sp.dma_start(f32(xnbr[part, :]), headsplit[b, x_]).then_inc(S["nbr_in"], 16)

            def load_rows(b, h):
                sp.dma_start(xr[:, h], x_v[b, h]).then_inc(S[f"xr_in{h}"], 16)

            load_neighbours(0)
            load_mix(0, 0)
            load_mix(0, 1)

            def store(b, h):
                sp.wait_ge(S["out_ok"], b * 2 + h + 1)
                sp.dma_start(o_v[b, h], xr[:, h]).then_inc(S[f"stored{h}"], 16)

            def graph(b, first, last):
                for h in range(2):
                    if not last:
                        sp.wait_ge(S["agg_lo_ok"], b * 4 + 2 * h + 2)
                        load_mix(b + 1, h)
                        if h == 1:
                            load_neighbours(b + 1)
                    if not first:
                        store(b - 1, h)
                        sp.wait_ge(S[f"stored{h}"], b * 16)
                    load_rows(b, h)

            graph(0, True, False)
            with sp.Fori(1, B - 1) as i:
                graph(i, False, False)
            graph(B - 1, False, True)
            for h in range(2):
                store(B - 1, h)
            for h in range(2):
                sp.wait_ge(S[f"stored{h}"], 16 * B)

        @block.tensor
        def _(pe):
            T_ = nc.tensor
            pe.wait_ge(S["const_in"], 16 * 7)
            T_.transpose(cp[:, 0:2 * KT], cw_rows[:], ident[0:2 * KT, 0:2 * KT]).then_inc(S["setup_t"], 1)
            pe.wait_ge(S["setup_v"], 5)

            def correct(unit, j):
                b, h = unit
                if j == 0:
                    if h == 0:
                        pe.wait_ge(S["nbr_in"], b * 128 + 128)
                    wait(pe, "agg_ok", upto(back(unit, 1), 2, 2))
                    wait(pe, "ms_ok", upto(back(unit, 2), 1, 1))
                else:
                    pe.wait_ge(S["agg_ok"], upto(unit, 2, 1))
                T_.matmul(cp[:], xnbr[:, j * P:(j + 1) * P], nbr[:, h * H:(h + 1) * H], start=True, stop=True)\
                    .then_inc(S["corr_psum"], 1)

            def hidden(unit, t):
                h = unit[1]
                if t == 0:
                    pe.wait_ge(S["agg_lo_ok"], upto(unit, 2, 2))
                wait(pe, "hb_ok", upto(unit, KT, t - 1))
                cols = slice(t * P, (t + 1) * P)
                for j in range(DT):
                    last = split_matmuls(nc, hp[t % 2][:], v1_hi[:, j, cols], v1_lo[:, j, cols],
                                         agg_hi[:, h, j, :], agg_lo[:, h, j, :], j == 0, j == DT - 1)
                last.then_inc(S["hid_psum"], 1)

            def sums(unit, next_too):
                pe.wait_ge(S["ss_ok"], upto(unit, KT - 1, KT - 1))
                pe.wait_ge(S["agg_ok"], upto(back(unit, -1) if next_too else unit, 2, 2))
                for r in range(RT):
                    last = T_.matmul(cp[:, r:r + 1], ssum[:, unit[1], r * P:(r + 1) * P], ones[:, 0:1], start=True, stop=True)
                last.then_inc(S["sum_psum"], 1)

            def spread(unit):
                pe.wait_ge(S["rd_ok"], upto(unit, 1, 1))
                wait(pe, "t_ok", upto(back(unit, 1), KT, KT))
                T_.matmul(rb[:], ones[:], rdiag[:].rearrange("p r c -> p (r c)"), start=True, stop=True)\
                    .then_inc(S["rb_psum"], 1)

            def output(unit, k):
                h = unit[1]
                pe.wait_ge(S["s_lo_ok"], upto(unit, KT, k + 1))
                if k == 0:
                    wait(pe, "y_ok", upto(back(unit, 2), 2, 2))
                for r in range(RT):
                    cols = slice(r * P, (r + 1) * P)
                    last = split_matmuls(nc, op[h][r // 2][:, (r % 2) * D:(r % 2 + 1) * D],
                                         s_hi[:, k % SR, cols], s_lo[:, k % SR, cols], v2_hi[:, k, :], v2_lo[:, k, :],
                                         k == 0 and r % 2 == 0, k == KT - 1, group=False)
                last.then_inc(S["o_step"], 1)

            def step(unit, j, cur, prev, nxt):
                if cur:
                    hidden(unit, j)
                if prev[0] and j == 1:
                    sums(back(unit, 1), cur)
                if prev[0] and j == 4:
                    spread(back(unit, 1))
                if late := lagging(unit, j, LAG, prev):
                    output(*late)
                if nxt and j in (3, 4):
                    correct(back(unit, -1), j - 3)

            correct((0, 0), 0)
            correct((0, 0), 1)
            walk(pe, step)

        @block.scalar
        def _(act):
            A = nc.scalar.activation
            act.wait_ge(S["const_in"], 16 * 7)
            A(v1_hi[:], raw[:, 0:DT * HID].rearrange("p (k n) -> p k n", k=DT), ACT.Copy).then_inc(S["setup_a"], 1)
            A(v2_hi[:], raw[:, DT * HID:DT * HID + KT * D].rearrange("p (k n) -> p k n", k=KT), ACT.Copy)\
                .then_inc(S["setup_a"], 1)
            act.wait_ge(S["setup_v"], 5)

            def agg_high(unit, j):
                h = unit[1]
                act.wait_ge(S["agg_ok"], upto(unit, 2, j + 1))
                A(agg_hi[:, h, j, :], mix[:, h, j, :], ACT.Copy).then_inc(S["agg_hi_ok"], 1)

            def hidden(unit, t):
                h = unit[1]
                act.wait_ge(S["hid_psum"], upto(unit, KT, t + 1))
                A(hb[:, h, t, :], hp[t % 2][:], ACT.Identity, bias=cw[:, t:t + 1]).then_inc(S["hb_ok"], 1)
                wait(act, "ss_ok", upto(unit, KT - 1, t - SR) if t > SR else
                     upto(unit, KT - 1, 1) if t == SR else upto(back(unit, 1), KT - 1, t + KT - SR))
                act.wait_ge(S["hb_ok"], upto(unit, KT, t + 1))
                A(sq[:, t % SR, :], hb[:, h, t, :], ACT.Square).then_inc(S["sq_ok"], 1)

            def silu(unit, k):
                h = unit[1]
                act.wait_ge(S["t_ok"], upto(unit, KT, k + 1))
                A(hb[:, h, k, :], hb[:, h, k, :], ACT.Silu, scale=cw[:, KT + k:KT + k + 1]).then_inc(S["silu_ok"], 1)
                wait(act, "o_step", upto(unit, KT, k + 1 - SR))
                act.wait_ge(S["silu_ok"], upto(unit, KT, k + 1))
                A(s_hi[:, k % SR, :], hb[:, h, k, :], ACT.Copy).then_inc(S["s_hi_ok"], 1)

            def step(unit, j, cur, prev, nxt):
                if nxt and j in (5, 6):
                    agg_high(back(unit, -1), j - 5)
                if late := lagging(unit, j, LAG - 1, prev):
                    silu(*late)
                if cur:
                    hidden(unit, j)

            agg_high((0, 0), 0)
            agg_high((0, 0), 1)
            walk(act, step)

        @block.vector
        def _(dve):
            V = nc.vector
            dve.wait_ge(S["const_in"], 16 * 7)
            V.memset(half[:], -0.5).then_inc(S["setup_v"], 1)
            V.memset(ones[:], 1.0).then_inc(S["setup_v"], 1)
            dve.wait_ge(S["setup_a"], 2)
            V.tensor_tensor(v1_lo[:], raw[:, 0:DT * HID].rearrange("p (k n) -> p k n", k=DT), f32(v1_hi[:]), ALU.subtract)\
                .then_inc(S["setup_v"], 1)
            V.tensor_tensor(v2_lo[:], raw[:, DT * HID:DT * HID + KT * D].rearrange("p (k n) -> p k n", k=KT), f32(v2_hi[:]),
                            ALU.subtract).then_inc(S["setup_v"], 1)
            dve.wait_ge(S["setup_t"], 1)
            V.tensor_copy(cw[:], cp[:, 0:2 * KT]).then_inc(S["setup_v"], 1)
            dve.wait_ge(S["setup_v"], 5)

            def aggregate(unit, j):
                b, h = unit
                if j == 0:
                    dve.wait_ge(S[f"mix_in{h}"], b * 16 + 16)
                dve.wait_ge(S["corr_psum"], upto(unit, 2, j + 1))
                V.tensor_tensor(mix[:, h, j, :], cp[:], mix[:, h, j, :], ALU.add).then_inc(S["agg_ok"], 1)

            def mean_square(unit):
                dve.wait_ge(S["sum_psum"], upto(unit, 1, 1))
                V.tensor_scalar(ms[:], cp[:, 0:RT], 1.0 / HID, RMS_EPS, ALU.mult, ALU.add).then_inc(S["ms_ok"], 1)

            def diagonals(unit):
                dve.wait_ge(S["rr_ok"], upto(unit, 1, 1))
                for r in range(RT):
                    last = V.tensor_scalar(rdiag[:, r, :], ident[:], rr[:, r:r + 1], None, ALU.mult)
                last.then_inc(S["rd_ok"], 1)

            def scale(unit, k):
                h = unit[1]
                if k == 0:
                    dve.wait_ge(S["rb_psum"], upto(unit, 1, 1))
                    dve.wait_ge(S["sq_ok"], upto(unit, KT, KT))
                V.tensor_tensor(hb[:, h, k, :], rb[:], hb[:, h, k, :], ALU.mult).then_inc(S["t_ok"], 1)

            def silu_low(unit, k):
                dve.wait_ge(S["s_hi_ok"], upto(unit, KT, k + 1))
                V.tensor_tensor(s_lo[:, k % SR, :], hb[:, unit[1], k, :], f32(s_hi[:, k % SR, :]), ALU.subtract)\
                    .then_inc(S["s_lo_ok"], 1)

            def residual(unit):
                h = unit[1]
                dve.wait_ge(S["o_step"], upto(unit, KT, KT))
                dve.wait_ge(S["xb_ok"], upto(unit, 2, 2))
                for i in range(2):
                    rows = xr[:, h, 2 * i:2 * i + 2, :].rearrange("p r d -> p (r d)")
                    V.tensor_tensor(rows, op[h][i][:], rows, ALU.add).then_inc(S["y_ok"], 1)
                for r in range(RT):
                    if r % 2 == 0:
                        dve.wait_ge(S["y_ok"], upto(unit, 2, r // 2 + 1))
                    last = V.bn_stats(stats[:, r, :], xr[:, h, r, :])
                last.then_inc(S["st_ok"], 1)

            def variances(unit):
                dve.wait_ge(S["st_ok"], upto(unit, 1, 1))
                V.memset(spacer[:], 0.0)
                for r in range(RT):
                    last = V.bn_aggr(mean_var[:, r, :], stats[:, r, :])
                last.then_inc(S["mv_ok"], 1)
                dve.wait_ge(S["mv_ok"], upto(unit, 1, 1))
                V.tensor_scalar(var_eps[:], mean_var[:, :, 1], LN_EPS, None, ALU.add).then_inc(S["ve_ok"], 1)

            def normalise(unit):
                h = unit[1]
                dve.wait_ge(S["pw_ok"], upto(unit, 1, 1))
                for r in range(RT):
                    last = V.tensor_scalar(xr[:, h, r, :], xr[:, h, r, :], mean_var[:, r, 0:1], rstd[:, r:r + 1],
                                           ALU.subtract, ALU.mult)
                last.then_inc(S["out_ok"], 1)

            def step(unit, j, cur, prev, nxt):
                if nxt and j in (4, 5):
                    aggregate(back(unit, -1), j - 4)
                if prev[0] and j == 2:
                    mean_square(back(unit, 1))
                if prev[0] and j == 4:
                    diagonals(back(unit, 1))
                if late := lagging(unit, j, LAG, prev):
                    silu_low(*late)
                if late := lagging(unit, j, LAG - 1, prev):
                    scale(*late)
                if prev[1] and j == 5:
                    residual(back(unit, 2))
                if prev[1] and j == 6:
                    variances(back(unit, 2))
                if prev[1] and j == 7:
                    normalise(back(unit, 2))

            aggregate((0, 0), 0)
            aggregate((0, 0), 1)
            walk(dve, step)

        @block.gpsimd
        def _(pool):
            G = nc.gpsimd
            pool.wait_ge(S["setup_v"], 5)

            def agg_low(unit, j):
                h = unit[1]
                pool.wait_ge(S["agg_hi_ok"], upto(unit, 2, j + 1))
                G.tensor_tensor(agg_lo[:, h, j, :], mix[:, h, j, :], f32(agg_hi[:, h, j, :]), ALU.subtract)\
                    .then_inc(S["agg_lo_ok"], 1)

            def add_squares(unit, t):
                h = unit[1]
                pool.wait_ge(S["sq_ok"], upto(unit, KT, t + 1))
                if t > 1:
                    pool.wait_ge(S["ss_ok"], upto(unit, KT - 1, t - 1))
                G.tensor_tensor(ssum[:, h, :], sq[:, 0, :] if t == 1 else ssum[:, h, :], sq[:, t % SR, :], ALU.add)\
                    .then_inc(S["ss_ok"], 1)

            def inverse_rms(unit):
                pool.wait_ge(S["ms_ok"], upto(unit, 1, 1))
                G.tensor_tensor(rr[:], ms[:], half[:], ALU.pow).then_inc(S["rr_ok"], 1)

            def add_bias(unit, i):
                b, h = unit
                if i == 0:
                    pool.wait_ge(S[f"xr_in{h}"], b * 16 + 16)
                rows = xr[:, h, 2 * i:2 * i + 2, :]
                G.tensor_tensor(rows, rows, c2_bc[:], ALU.add).then_inc(S["xb_ok"], 1)

            def inverse_deviation(unit):
                pool.wait_ge(S["ve_ok"], upto(unit, 1, 1))
                G.tensor_tensor(rstd[:], var_eps[:], half[:], ALU.pow).then_inc(S["pw_ok"], 1)

            def step(unit, j, cur, prev, nxt):
                if nxt and j in (5, 6):
                    agg_low(back(unit, -1), j - 5)
                if prev[0] and j == 2:
                    inverse_rms(back(unit, 1))
                if prev[1] and j in (2, 3):
                    add_bias(back(unit, 2), j - 2)
                if prev[1] and j == 6:
                    inverse_deviation(back(unit, 2))
                if cur and j > 0:
                    add_squares(unit, j)

            agg_low((0, 0), 0)
            agg_low((0, 0), 1)
            walk(pool, step)


def program(nc, x, adj, nodemask, w0t, b0, w1, b1, g_w1, g_b1, g_w2, g_b2, fusion, eps, v1, c1, rms_w, v2, c2,
            eye, same, place, out):
    B, N, D = x.shape
    mixed = nc.dram_tensor("mixed_scratch", (B, P, 4, N // 2), F32).ap()
    x3 = nc.dram_tensor("x3_scratch", (B, N, D), F32).ap()
    nbr25 = nc.dram_tensor("nbr25_scratch", (B, 2, NODES, N), F32).ap()
    x2head = nc.dram_tensor("x2head_scratch", (B, NODES, D), F32).ap()
    headsplit = nc.dram_tensor("head_scratch", (B, 2, NODES, D), F32).ap()
    part1(nc, x, adj, nodemask, w0t, b0, w1, b1, eps, eye, mixed, x3, nbr25, x2head)
    part2(nc, adj, x2head, g_w1, g_b1, g_w2, g_b2, fusion, eye, same, place, x3, headsplit)
    part3(nc, mixed, x3, nbr25, headsplit, v1, c1, rms_w, v2, c2, eye, out)


def kernel(x, adj, nodemask, L0_gnn_W, L0_gnn_b, L1_gnn_weight, L1_gnn_bias, L2_gnn_W1, L2_gnn_b1, L2_gnn_W2,
           L2_gnn_b2, L2_gnn_fusion_w, L3_gnn_epsilon, L3_gnn_W1, L3_gnn_b1, L3_gnn_rms_weight, L3_gnn_W2, L3_gnn_b2):
    import concourse.bacc as bacc
    from concourse.bass_utils import run_bass_kernel_spmd

    eye, same, place = layout_constants(x.shape[0])
    arrays = {
        "x": x, "adj": adj, "nodemask": nodemask, "w0t": np.asarray(L0_gnn_W).T, "b0": L0_gnn_b,
        "w1": L1_gnn_weight, "b1": L1_gnn_bias, "g_w1": L2_gnn_W1, "g_b1": L2_gnn_b1, "g_w2": L2_gnn_W2,
        "g_b2": L2_gnn_b2, "fusion": L2_gnn_fusion_w, "eps": np.asarray(L3_gnn_epsilon).reshape(1),
        "v1": L3_gnn_W1, "c1": L3_gnn_b1, "rms_w": L3_gnn_rms_weight, "v2": L3_gnn_W2, "c2": L3_gnn_b2,
        "eye": eye, "same": same, "place": place,
    }
    arrays = {n: np.ascontiguousarray(a) for n, a in arrays.items()}
    nc = bacc.Bacc("TRN2", target_bir_lowering=False, num_devices=1)
    args = {n: nc.dram_tensor("in_" + n, a.shape, F32, kind="ExternalInput").ap() for n, a in arrays.items()}
    out = nc.dram_tensor("out", x.shape, F32, kind="ExternalOutput").ap()
    program(nc, **args, out=out)
    r = run_bass_kernel_spmd(nc, [{"in_" + n: a for n, a in arrays.items()}], core_ids=[0])
    return r.results[0]["out"]
```

```python
from contextlib import ExitStack

import numpy as np

import concourse.bass as bass
from concourse import mybir
from concourse.alu_op_type import AluOpType as ALU

F32 = mybir.dt.float32
F32R = mybir.dt.float32r
ACT = mybir.ActivationFunctionType

P = 128
LN_EPS = 1e-5
DEG_EPS = 1e-8
QUANT = 0.01
RMS_EPS = 1e-6
GROUPS = [list(range(25)), [0, 1, 2, 3, 4, 5, 6, 7, 8], [0, 9, 10, 11, 12, 13, 14],
          [6, 7, 8, 12, 13, 14], [3, 4, 5, 9, 10, 11]]
NODES = 25
NEAR = 32


class Held:
    pass


def f32(ap):
    return ap.bitcast(F32)


def split_matmuls(nc, out, w_hi, w_lo, m_hi, m_lo, first, last, group=True):
    nc.tensor.matmul(out, w_hi, m_hi, start=first, stop=False, skip_group_check=not group)
    nc.tensor.matmul(out, w_hi, m_lo, start=False, stop=False, skip_group_check=not group)
    return nc.tensor.matmul(out, w_lo, m_hi, start=False, stop=last, skip_group_check=not group)


def open_shared(ctx, nc, B, N, D):
    NT = len(group_tiles(B))
    T = N // P
    sh = Held()

    def sb(name, shape):
        return ctx.enter_context(nc.sbuf_tensor(name, shape, F32))

    sh.a_rows = sb("a_rows", [P, T * N])
    sh.x_rows = sb("x_rows", [P, max(T, NT) * D])
    sh.mix = sb("mix", [P, 4 * (N // 2)])
    sh.ident = sb("ident", [P, P])
    sh.cadj = sb("cadj", [P, NT, NODES])
    sh.same = sb("same_sb", [P, NT, 16])
    sh.S = {n: ctx.enter_context(nc.semaphore("sh_" + n)) for n in
            ["w_in0", "w_in1", "w_in2", "w_in3", "adj_in", "rows_in", "mix_out", "nodes_out0", "nodes_out1"]}
    return sh


def part1(nc, sh, x, adj, nodemask, w0t, b0, w1, b1, eps, eye, mixed, x3, near_at, x2head, preload_weights, preload_rows):
    B, N, D = x.shape
    T = N // P
    DT = D // P
    H = N // 2
    TH = T // 2
    R = 4
    assert H == 512 and D == 256 and T == 8

    with ExitStack() as ctx:
        def sb(name, shape, dt=F32):
            return ctx.enter_context(nc.sbuf_tensor(name, shape, dt))

        def ps(name, shape):
            return ctx.enter_context(nc.psum_tensor(name, shape, F32))

        def sem(name):
            return ctx.enter_context(nc.semaphore(name))

        at_hi, at_lo = sb("at_hi", [P, T, N], F32R), sb("at_lo", [P, T, N], F32R)
        a_rows = sh.a_rows[:].rearrange("p (t n) -> p t n", t=T)
        x_in = sh.x_rows[:, 0:T * D].rearrange("p (t d) -> p t d", t=T)
        xres = sb("xres", [P, T, D])
        sup = sb("sup", [P, T, D])
        mv0_hi, mv0_lo = sb("mv0_hi", [P, T * D], F32R), sb("mv0_lo", [P, T * D], F32R)
        x1_hi, x1_lo = sb("x1_hi", [P, T, D], F32R), sb("x1_lo", [P, T, D], F32R)
        x3_hi, x3_lo = sb("x3_hi", [P, T, D], F32R), sb("x3_lo", [P, T, D], F32R)
        mix_sb = sh.mix[:].rearrange("p (j n) -> p j n", j=2 * DT)
        xt_hi, xt_lo = sb("xt_hi", [P, 2, DT, P], F32R), sb("xt_lo", [P, 2, DT, P], F32R)
        row = sb("row", [P, R, D])
        diag = sb("diag", [P, T, P])
        junk = sb("junk", [P, N], mybir.dt.bfloat16)
        head = sb("head", [NODES, D])
        ident, epsi = sh.ident, sb("epsi", [P, P])
        w0_hi, w0_lo = sb("w0_hi", [P, DT, D], F32R), sb("w0_lo", [P, DT, D], F32R)
        dw = sb("dw", [P, DT, D], F32R)
        b0_bc, b1_bc = sb("b0_bc", [P, D]), sb("b1_bc", [P, D])
        masks = sb("masks", [P, B * T])
        degs, dis, dism = sb("degs", [P, T]), sb("dis", [P, T]), sb("dism", [P, T])
        minus_half = sb("minus_half", [P, T])
        stats = sb("stats", [P, 4, 6])
        mean_var = sb("mean_var", [P, 3 * T + 6, 2])
        ln_eps = sb("ln_eps", [P, 2])
        var_eps, rstd = sb("var_eps", [P, 3 * T + 6]), sb("rstd", [P, 3 * T + 6])
        eps_sb, spacer = sb("eps_sb", [P, 1]), sb("spacer", [P, 3])
        tail = sb("tail", [P, 1])
        w_stage = sup

        tr = [ps(f"tr{i}", [P, H]) for i in range(2)]
        nt = [ps(f"nt{i}", [P, D]) for i in range(2)]
        acc = [ps(f"acc{i}", [P, H]) for i in range(4)]

        names = ["consts", "a_loaded0", "a_loaded1", "a_loaded2", "a_loaded3", "x_loaded", "head_out", "nbr_out", "x3_out",
                 "setup_v", "setup_a", "setup_t",
                 "transposed", "at_hi_ok", "at_lo_ok", "xt_hi_ok", "xt_lo_ok",
                 "sup_psum", "sup_ok", "mv_hi_ok", "mv_lo_ok", "deg_sum", "deg_ok", "dis_pow", "dism_ok",
                 "m0_psum", "row0_ok", "relu0_ok", "y0_ok", "st0_a", "st0_b", "var0_ok", "pow0_ok",
                 "x1_ok", "x1_hi_ok", "x1_lo_ok",
                 "z_psum", "z_hi_ok", "z_lo_ok", "diag_ok", "at_hi_eps", "at_lo_eps",
                 "m1_psum", "row1_ok", "relu1_ok", "y1_ok", "st1_a", "st1_b", "ve_ok", "pow_ok",
                 "x2_ok", "head_ok", "st2_a", "st2_b", "x3_ok", "x3_hi_ok",
                 "x3_lo_ok", "x3_lo0", "mix_psum", "mix_ok"]
        S = {n: sem("p1_" + n) for n in names}
        S["mix_out"] = sh.S["mix_out"]

        first_ring = tr + acc

        def var_col(layer, n):
            c = n if layer == 0 else T + 2 * (n + layer) + layer - 3
            return slice(c, c + 1)

        def diag_tiles(at, half):
            flat = at[:].rearrange("p k n -> p (k n)")
            even = flat[:, 0:(T - 1) * (N + P)].rearrange("p (k w) -> p k w", k=T - 1)
            if half == 0:
                return [(even[:, 0:TH, 0:P], slice(0, TH))]
            return [(even[:, TH:T - 1, 0:P], slice(TH, T - 1)),
                    (at[:, T - 1:T, (T - 1) * P:T * P], slice(T - 1, T))]

        block = ctx.enter_context(nc.Block("part1"))

        a_v = adj.rearrange("b (t p) m -> b p t m", p=P)
        x_v = x.rearrange("b (t p) d -> b p t d", p=P)
        x3_v = x3.rearrange("b (t p) d -> b p t d", p=P)

        @block.sync
        def _(sp):
            sp.dma_start(ident[:], eye).then_inc(S["consts"], 16)
            sp.dma_start(w_stage[:, 0:DT, :], w0t.rearrange("(k p) o -> p k o", p=P)).then_inc(S["consts"], 16)
            sp.dma_start(w_stage[:, DT:2 * DT, :], w1.rearrange("(k p) o -> p k o", p=P)).then_inc(S["consts"], 16)
            sp.dma_start(b0_bc[:], b0.rearrange("(a d) -> a d", a=1).broadcast_to([P, D])).then_inc(S["consts"], 16)
            sp.dma_start(b1_bc[:], b1.rearrange("(a d) -> a d", a=1).broadcast_to([P, D])).then_inc(S["consts"], 16)
            sp.dma_start(eps_sb[:], eps.rearrange("(a d) -> a d", a=1).broadcast_to([P, 1])).then_inc(S["consts"], 16)
            sp.dma_start(row[0:B * T, 0, 0:P], nodemask.rearrange("b (t p) -> (b t) p", p=P)).then_inc(S["consts"], 16)

            def load_adjacency(b):
                for q in range(4):
                    sp.dma_start(a_rows[:, 2 * q:2 * q + 2, :], a_v[b, :, 2 * q:2 * q + 2, :]).then_inc(S[f"a_loaded{q}"], 16)

            def load_features(b):
                sp.dma_start(x_in, x_v[b]).then_inc(S["x_loaded"], 16)

            load_features(0)
            load_adjacency(0)

            def graph(b, more):
                sp.wait_ge(S["transposed"], b * 3 * T + 3 * T)
                sp.wait_ge(S["deg_sum"], b * T + T)
                if more:
                    load_adjacency(b + 1)
                else:
                    preload_weights(sp)
                sp.wait_ge(S["y0_ok"], b * T + T)
                if more:
                    load_features(b + 1)
                sp.wait_ge(S["at_hi_eps"], b * 2 + 1)
                sp.wait_ge(S["at_lo_eps"], b * 2 + 1)
                sp.dma_start(near_at[b, 0], f32(at_hi[0:NEAR, 0, :])).then_inc(S["nbr_out"], 16)
                sp.dma_start(near_at[b, 1], f32(at_lo[0:NEAR, 0, :])).then_inc(S["nbr_out"], 16)
                sp.wait_ge(S["head_ok"], b + 1)
                sp.dma_start(x2head[b], head[:]).then_inc(S["head_out"], 16)
                if not more:
                    sp.wait_ge(S["head_out"], 16 * B + 16)
                    preload_rows(sp)
                for half in range(2):
                    sp.wait_ge(S["x3_ok"], b * T + TH * (half + 1))
                    rows = slice(TH * half, TH * (half + 1))
                    sp.dma_start(x3_v[b, :, rows, :], xres[:, rows, :]).then_inc(S["x3_out"], 16)
                sp.wait_ge(S["mix_ok"], b * 4 + 4)
                sp.dma_start(mixed[b], mix_sb).then_inc(S["mix_out"], 16)

            with sp.Fori(0, B - 1) as i:
                graph(i, True)
            graph(B - 1, False)
            sp.wait_ge(S["nbr_out"], 32 * B)
            sp.wait_ge(S["x3_out"], 32 * B + 32)

        @block.tensor
        def _(pe):
            pe.wait_ge(S["consts"], 16 * 7)
            nc.tensor.transpose(tr[0][:, 0:B * T], row[0:B * T, 0, 0:P], ident[0:B * T, 0:B * T]).then_inc(S["setup_t"], 1)
            pe.wait_ge(S["setup_v"], 7)

            def transpose_a(b, k, half, after):
                if half == 1:
                    pe.wait_ge(S["at_lo_ok"], b * 2 * T + 2 * k + 1)
                elif after or k > 0:
                    pe.wait_ge(S["xt_lo_ok"], b * T + k)
                if k == 0:
                    for q in (2 * half, 2 * half + 1):
                        pe.wait_ge(S[f"a_loaded{q}"], b * 16 + 16)
                for j in range(4):
                    last = nc.tensor.transpose(tr[(3 * k + 2 * half) % 2][:, j * P:(j + 1) * P],
                                               a_rows[:, 4 * half + j, k * P:(k + 1) * P], ident[:])
                last.then_inc(S["transposed"], 1)

            def transpose_x(b, k, after):
                if after or k > 0:
                    pe.wait_ge(S["at_lo_ok"], b * 2 * T + 2 * k)
                if k == 0:
                    pe.wait_ge(S["x_loaded"], b * 16 + 16)
                for j in range(DT):
                    last = nc.tensor.transpose(tr[(3 * k + 1) % 2][:, j * P:(j + 1) * P],
                                               x_in[:, k, j * P:(j + 1) * P], ident[:])
                last.then_inc(S["transposed"], 1)

            def support0(b, k, after):
                pe.wait_ge(S["xt_hi_ok"], b * T + k + 1)
                pe.wait_ge(S["xt_lo_ok"], b * T + k + 1)
                if k >= 2:
                    pe.wait_ge(S["sup_ok"], b * T + k - 1)
                elif after:
                    pe.wait_ge(S["row1_ok"], b * T - 2 + k + 1)
                for j in range(DT):
                    last = split_matmuls(nc, nt[k % 2][:], xt_hi[:, k % 2, j, :], xt_lo[:, k % 2, j, :],
                                         w0_hi[:, j, :], w0_lo[:, j, :], j == 0, j == DT - 1)
                last.then_inc(S["sup_psum"], 1)

            def first_graph():
                def free(use):
                    if use < 0:
                        return
                    if use >= 2 * T:
                        pe.wait_ge(S["at_lo_ok"], use - T + 1)
                    else:
                        pe.wait_ge(S[("at_lo_ok", "xt_lo_ok")[use % 2]], use // 2 + 1)

                def transposes(use, src, tiles):
                    free(use - len(first_ring))
                    for j in range(tiles):
                        last = nc.tensor.transpose(first_ring[use % len(first_ring)][:, j * P:(j + 1) * P], src(j), ident[:])
                    last.then_inc(S["transposed"], 1)

                for q in range(2):
                    pe.wait_ge(S[f"a_loaded{q}"], 16)
                for k in range(T):
                    transposes(2 * k, lambda j: a_rows[:, j, k * P:(k + 1) * P], TH)
                    if k == 0:
                        pe.wait_ge(S["x_loaded"], 16)
                    transposes(2 * k + 1, lambda j: x_in[:, k, j * P:(j + 1) * P], DT)
                    if k > 0:
                        support0(0, k - 1, False)
                support0(0, T - 1, False)
                for q in range(2, 4):
                    pe.wait_ge(S[f"a_loaded{q}"], 16)
                for k in range(T):
                    transposes(2 * T + k, lambda j: a_rows[:, TH + j, k * P:(k + 1) * P], TH)
                pe.wait_ge(S["at_lo_ok"], 2 * T)

            def layer0(b):
                for n in range(T):
                    if n < 2:
                        pe.wait_ge(S["sup_ok"], b * T + T - 1 + n)
                    else:
                        pe.wait_ge(S["row0_ok"], b * T + n - 1)
                    for k in range(T):
                        if n == 0:
                            pe.wait_ge(S["mv_lo_ok"], b * T + k + 1)
                            pe.wait_ge(S["at_lo_ok"], b * 2 * T + 2 * k + 2)
                        cols = slice(n * P, (n + 1) * P)
                        last = split_matmuls(nc, nt[n % 2][:], at_hi[:, k, cols], at_lo[:, k, cols],
                                             mv0_hi[:, k * D:(k + 1) * D], mv0_lo[:, k * D:(k + 1) * D],
                                             k == 0, k == T - 1)
                    last.then_inc(S["m0_psum"], 1)

            def support1(b, n):
                if n % TH == 0:
                    pe.wait_ge(S["z_lo_ok"], b * 4 + 2 * (n // TH) + 2)
                if n < 2:
                    pe.wait_ge(S["row0_ok"], b * T + T - 1 + n)
                else:
                    pe.wait_ge(S["row1_ok"], b * T + n - 1)
                for j in range(DT):
                    cols = slice(j * N + n * P, j * N + (n + 1) * P)
                    nc.tensor.matmul(nt[n % 2][:], mv0_hi[:, cols], dw[:, j, :], start=j == 0, stop=False)
                    last = nc.tensor.matmul(nt[n % 2][:], mv0_lo[:, cols], dw[:, j, :], start=False, stop=j == DT - 1)
                last.then_inc(S["m1_psum"], 1)

            def layer1(b):
                for half in range(2):
                    for k in range(T):
                        if half == 0:
                            pe.wait_ge(S["x1_lo_ok"], b * T + k + 1)
                        for j in range(DT):
                            last = split_matmuls(nc, acc[2 * half + j][:],
                                                 x1_hi[:, k, j * P:(j + 1) * P], x1_lo[:, k, j * P:(j + 1) * P],
                                                 at_hi[:, k, half * H:(half + 1) * H], at_lo[:, k, half * H:(half + 1) * H],
                                                 k == 0, k == T - 1)
                            if k == T - 1:
                                last.then_inc(S["z_psum"], 1)
                        if half == 1 and 1 <= k <= TH:
                            support1(b, k - 1)

            def layer3_sum(b, k, half, j):
                if half == 0 and j == 0:
                    if k == 0:
                        pe.wait_ge(S["x3_lo0"], b + 1)
                    else:
                        pe.wait_ge(S["x3_lo_ok"], b * (T - 1) + k)
                    if k % TH == 0:
                        pe.wait_ge(S["at_hi_eps"], b * 2 + k // TH + 1)
                        pe.wait_ge(S["at_lo_eps"], b * 2 + k // TH + 1)
                last = split_matmuls(nc, acc[2 * half + j][:],
                                     x3_hi[:, k, j * P:(j + 1) * P], x3_lo[:, k, j * P:(j + 1) * P],
                                     at_hi[:, k, half * H:(half + 1) * H], at_lo[:, k, half * H:(half + 1) * H],
                                     k == 0, k == T - 1)
                if k == T - 1:
                    last.then_inc(S["mix_psum"], 1)

            def layer3_and_prepare(b, more):
                for k in range(T):
                    layer3_sum(b, k, 0, 0)
                    layer3_sum(b, k, 0, 1)
                    if more:
                        transpose_a(b + 1, k, 0, True)
                    if k == 0:
                        for n in range(TH, T):
                            support1(b, n)
                    layer3_sum(b, k, 1, 0)
                    if more:
                        transpose_x(b + 1, k, True)
                    layer3_sum(b, k, 1, 1)
                    if more:
                        transpose_a(b + 1, k, 1, True)
                        if k > 0:
                            support0(b + 1, k - 1, True)
                if more:
                    support0(b + 1, T - 1, True)

            first_graph()
            with pe.Fori(0, B - 1) as i:
                layer0(i)
                layer1(i)
                layer3_and_prepare(i, True)
            layer0(B - 1)
            layer1(B - 1)
            layer3_and_prepare(B - 1, False)

        @block.scalar
        def _(act):
            act.wait_ge(S["consts"], 16 * 7)
            nc.scalar.activation(w0_hi[:], w_stage[:, 0:DT, :], ACT.Copy).then_inc(S["setup_a"], 1)
            nc.scalar.activation(epsi[:], ident[:], ACT.Copy, scale=eps_sb[:, 0:1]).then_inc(S["setup_a"], 1)

            def row_sum(b, t, first=False):
                if t % 2 == 0:
                    act.wait_ge(S[f"a_loaded{t // 2}"], b * 16 + 16)
                if not first:
                    act.wait_ge(S["deg_sum"], b * T + t)
                nc.scalar.activation(junk[:], a_rows[:, t, :], ACT.Copy, accum_out=degs[:, t:t + 1])\
                    .then_inc(S["deg_sum"], 1)

            def a_high(b, k, half):
                act.wait_ge(S["transposed"], b * 3 * T + 3 * k + 2 * half + 1)
                nc.scalar.activation(at_hi[:, k, half * H:(half + 1) * H], tr[(3 * k + 2 * half) % 2][:], ACT.Copy)\
                    .then_inc(S["at_hi_ok"], 1)

            def prepare(b, k, x3_step=None, begun=False):
                for use, half in enumerate((0, None, 1)):
                    if use == (2 if begun else 1) and x3_step is not None:
                        chain(b - 1, x3_step)
                    if use == 1 and 1 < k <= T + 1:
                        if k == 2:
                            act.wait_ge(S["dism_ok"], b + 1)
                        act.wait_ge(S["sup_ok"], b * T + k - 1)
                        nc.scalar.activation(mv0_hi[:, (k - 2) * D:(k - 1) * D], sup[:, k - 2, :], ACT.Copy,
                                             scale=dis[:, k - 2:k - 1]).then_inc(S["mv_hi_ok"], 1)
                    if k < T:
                        if half is None:
                            act.wait_ge(S["transposed"], b * 3 * T + 3 * k + 2)
                            if k >= 2:
                                act.wait_ge(S["sup_psum"], b * T + k - 1)
                            nc.scalar.activation(xt_hi[:, k % 2], tr[(3 * k + 1) % 2][:, 0:D]
                                                 .rearrange("p (j c) -> p j c", j=DT), ACT.Copy).then_inc(S["xt_hi_ok"], 1)
                        elif half == 1 or not begun:
                            a_high(b, k, half)

            def z_high(b, half):
                for j in range(DT):
                    act.wait_ge(S["z_psum"], b * 4 + 2 * half + j + 1)
                    nc.scalar.activation(mv0_hi[:, j * N + half * H:j * N + (half + 1) * H], acc[2 * half + j][:], ACT.Copy)\
                        .then_inc(S["z_hi_ok"], 1)

            def diag_high(b, half):
                act.wait_ge(S["diag_ok"], b * 4 + 4)
                for dst, tiles in diag_tiles(at_hi, half):
                    last = nc.scalar.activation(dst, diag[:, tiles, :], ACT.Copy)
                last.then_inc(S["at_hi_eps"], 1)

            def chain(b, s):
                n = s - 3
                if n == 0:
                    act.wait_ge(S["x2_ok"], b * T + 1)
                    act.wait_ge(S["head_out"], b * 16 + 16)
                    nc.scalar.activation(head[:], xres[0:NODES, 0, :], ACT.Copy).then_inc(S["head_ok"], 1)
                if 0 <= n < T:
                    act.wait_ge(S["x3_ok"], b * T + n + 1)
                    nc.scalar.activation(x3_hi[:, n, :], xres[:, n, :], ACT.Copy, scale=tail[:, 0:1] if n == 0 else 1.0)\
                        .then_inc(S["x3_hi_ok"], 1)

            def relu1(b, n):
                act.wait_ge(S["row1_ok"], b * T + n + 1)
                nc.scalar.activation(row[:, n % R, :], row[:, n % R, :], ACT.Relu).then_inc(S["relu1_ok"], 1)

            def graph(b, more):
                for s in range(T + 3):
                    if s < T:
                        act.wait_ge(S["row0_ok"], b * T + s + 1)
                        nc.scalar.activation(row[:, s % R, :], row[:, s % R, :], ACT.Relu, scale=dism[:, s:s + 1])\
                            .then_inc(S["relu0_ok"], 1)
                    n = s - 2
                    if 0 <= n < T:
                        act.wait_ge(S["x1_ok"], b * T + n + 1)
                        nc.scalar.activation(x1_hi[:, n, :], xres[:, n, :], ACT.Copy).then_inc(S["x1_hi_ok"], 1)
                if more:
                    for t in range(T - 3):
                        row_sum(b + 1, t)
                z_high(b, 0)
                diag_high(b, 0)
                if more:
                    row_sum(b + 1, T - 3)
                for s in range(TH + 1):
                    if s < TH:
                        relu1(b, s)
                    else:
                        z_high(b, 1)
                        if more:
                            row_sum(b + 1, T - 2)
                            act.wait_ge(S["nbr_out"], b * 32 + 32)
                            a_high(b + 1, 0, 0)
                            row_sum(b + 1, T - 1)
                        relu1(b, TH)
                    chain(b, s)
                for n in range(TH + 1, T):
                    relu1(b, n)
                for k in range(T + 2):
                    if more:
                        prepare(b + 1, k, TH + 1 + k, begun=k == 0)
                    else:
                        chain(b, TH + 1 + k)
                    if k == 1:
                        diag_high(b, 1)
                act.wait_ge(S["mix_out"], b * 16 + 16)
                for j in range(4):
                    act.wait_ge(S["mix_psum"], b * 4 + j + 1)
                    nc.scalar.activation(mix_sb[:, (j % 2) * 2 + j // 2, :], acc[j][:], ACT.Copy).then_inc(S["mix_ok"], 1)

            def scaled_high(n):
                act.wait_ge(S["sup_ok"], n + 1)
                nc.scalar.activation(mv0_hi[:, n * D:(n + 1) * D], sup[:, n, :], ACT.Copy, scale=dis[:, n:n + 1])\
                    .then_inc(S["mv_hi_ok"], 1)

            def first_graph():
                for t in range(TH):
                    row_sum(0, t, t == 0)
                for k in range(T):
                    act.wait_ge(S["transposed"], 2 * k + 1)
                    nc.scalar.activation(at_hi[:, k, 0:H], first_ring[2 * k % 6][:], ACT.Copy).then_inc(S["at_hi_ok"], 1)
                    act.wait_ge(S["transposed"], 2 * k + 2)
                    if k >= 2:
                        act.wait_ge(S["sup_psum"], k - 1)
                    nc.scalar.activation(xt_hi[:, k % 2], first_ring[(2 * k + 1) % 6][:, 0:D]
                                         .rearrange("p (j c) -> p j c", j=DT), ACT.Copy).then_inc(S["xt_hi_ok"], 1)
                    if k >= TH:
                        row_sum(0, k)
                for k in range(T):
                    act.wait_ge(S["transposed"], 2 * T + k + 1)
                    nc.scalar.activation(at_hi[:, k, H:N], first_ring[(2 * T + k) % 6][:], ACT.Copy).then_inc(S["at_hi_ok"], 1)
                    if k == 1:
                        act.wait_ge(S["dism_ok"], 1)
                    if k >= 1:
                        scaled_high(k - 1)
                scaled_high(T - 1)

            first_graph()
            act.wait_ge(S["setup_v"], 7)
            with act.Fori(0, B - 1) as i:
                graph(i, True)
            graph(B - 1, False)

        @block.vector
        def _(dve):
            V = nc.vector
            dve.wait_ge(S["consts"], 16 * 7)
            dve.wait_ge(S["setup_a"], 1)
            V.tensor_tensor(w0_lo[:], w_stage[:, 0:DT, :], f32(w0_hi[:]), ALU.subtract).then_inc(S["setup_v"], 1)
            V.tensor_scalar(dw[:], w_stage[:, DT:2 * DT, :], -QUANT, None, ALU.is_lt).then_inc(S["setup_v"], 1)
            dve.wait_ge(S["setup_v"], 2)
            V.scalar_tensor_tensor(dw[:], w_stage[:, DT:2 * DT, :], QUANT, f32(dw[:]), ALU.is_gt, ALU.subtract)\
                .then_inc(S["setup_v"], 1)
            V.memset(minus_half[:], -0.5).then_inc(S["setup_v"], 1)
            V.memset(ln_eps[:], LN_EPS)
            V.memset(tail[:], 1.0).then_inc(S["setup_v"], 1)
            dve.wait_ge(S["setup_v"], 5)
            V.memset(tail[0:NEAR, :], 0.0).then_inc(S["setup_v"], 1)
            dve.wait_ge(S["setup_t"], 1)
            V.tensor_copy(masks[:], tr[0][:, 0:B * T]).then_inc(S["setup_v"], 1)
            dve.wait_ge(S["setup_v"], 7)
            dve.wait_ge(S["setup_a"], 2)

            def degrees(b):
                dve.wait_ge(S["deg_sum"], b * T + T)
                V.tensor_scalar(degs[:], degs[:], 1.0, DEG_EPS, ALU.add, ALU.add).then_inc(S["deg_ok"], 1)

            def prepare(b, k, norms=None, begun=False):
                if k < T and not begun:
                    a_low(b, k, 0)
                if norms is not None:
                    chain_rows(b - 1, norms)
                if k < T:
                    dve.wait_ge(S["xt_hi_ok"], b * T + k + 1)
                    V.tensor_tensor(xt_lo[:, k % 2], tr[(3 * k + 1) % 2][:, 0:D].rearrange("p (j c) -> p j c", j=DT),
                                    f32(xt_hi[:, k % 2]), ALU.subtract).then_inc(S["xt_lo_ok"], 1)
                if norms is not None:
                    chain_variances(b - 1, norms)
                if k < T - 1:
                    a_low(b, k, 1)
                if 0 < k <= T:
                    dve.wait_ge(S["sup_psum"], b * T + k)
                    V.tensor_tensor(sup[:, k - 1, :], nt[(k - 1) % 2][:], b0_bc[:], ALU.add).then_inc(S["sup_ok"], 1)
                if k == T - 1:
                    a_low(b, k, 1)
                if 1 < k <= T + 1:
                    n = k - 2
                    dve.wait_ge(S["mv_hi_ok"], b * T + n + 1)
                    V.scalar_tensor_tensor(mv0_lo[:, n * D:(n + 1) * D], sup[:, n, :], dis[:, n:n + 1],
                                           f32(mv0_hi[:, n * D:(n + 1) * D]), ALU.mult, ALU.subtract)\
                        .then_inc(S["mv_lo_ok"], 1)

            def a_low(b, k, half):
                dve.wait_ge(S["at_hi_ok"], b * 2 * T + 2 * k + half + 1)
                cols = slice(half * H, (half + 1) * H)
                V.tensor_tensor(at_lo[:, k, cols], tr[(3 * k + 2 * half) % 2][:], f32(at_hi[:, k, cols]), ALU.subtract)\
                    .then_inc(S["at_lo_ok"], 1)

            def row_stats(b, n, ready, done):
                dve.wait_ge(S[ready], b * T + n + 1)
                V.bn_stats(stats[:, n % 4, :], xres[:, n, :]).then_inc(S[done], 1)

            def aggregate(b, n, layer, ready, done):
                dve.wait_ge(S[ready], b * T + n + 1)
                V.memset(spacer[:, layer:layer + 1], 0.0)
                V.bn_aggr(mean_var[:, var_col(layer, n), :], stats[:, n % 4, :]).then_inc(S[done], 1)

            def variance(b, n, ready, done):
                dve.wait_ge(S[ready], b * T + n + 1)
                V.tensor_scalar(var_eps[:, var_col(0, n)], mean_var[:, var_col(0, n), 1], LN_EPS, None, ALU.add)\
                    .then_inc(S[done], 1)

            def normalise(b, n, layer, powed, done):
                if powed:
                    dve.wait_ge(S[powed], b * T + n + 1)
                V.tensor_scalar(xres[:, n, :], xres[:, n, :], mean_var[:, var_col(layer, n), 0], rstd[:, var_col(layer, n)],
                                ALU.subtract, ALU.mult).then_inc(S[done], 1)

            def z_low(b, half):
                for j in range(DT):
                    dve.wait_ge(S["z_hi_ok"], b * 4 + 2 * half + j + 1)
                    cols = slice(j * N + half * H, j * N + (half + 1) * H)
                    V.tensor_tensor(mv0_lo[:, cols], acc[2 * half + j][:], f32(mv0_hi[:, cols]), ALU.subtract)\
                        .then_inc(S["z_lo_ok"], 1)

            def diag_low(b, half):
                dve.wait_ge(S["at_hi_eps"], b * 2 + half + 1)
                for (dst, tiles), (hi, _) in zip(diag_tiles(at_lo, half), diag_tiles(at_hi, half)):
                    last = V.tensor_tensor(dst, diag[:, tiles, :], f32(hi), ALU.subtract)
                last.then_inc(S["at_lo_eps"], 1)

            def row1(b, n):
                dve.wait_ge(S["m1_psum"], b * T + n + 1)
                V.scalar_tensor_tensor(row[:, n % R, :], nt[n % 2][:], QUANT, b1_bc[:], ALU.mult, ALU.add)\
                    .then_inc(S["row1_ok"], 1)

            def chain(b, s):
                chain_rows(b, s)
                chain_variances(b, s)

            def chain_rows(b, s):
                if 2 <= s < T + 3:
                    dve.wait_ge(S["pow_ok"], b * (T + 1) + s - 1)
                if 0 <= s - 2 < T:
                    normalise(b, s - 2, 1, None, "x2_ok")
                if 0 <= s - 3 < T:
                    if s == 3:
                        dve.wait_ge(S["head_ok"], b + 1)
                    normalise(b, s - 3, 2, None, "x3_ok")
                if 0 <= s - 2 < T:
                    row_stats(b, s - 2, "x2_ok", "st2_a")
                if 0 <= s - 1 < T:
                    row_stats(b, s - 1, "y1_ok", "st1_a")

            def chain_variances(b, s):
                if 0 <= s - 2 < T:
                    aggregate(b, s - 2, 2, "st2_a", "st2_b")
                if 0 <= s - 1 < T:
                    aggregate(b, s - 1, 1, "st1_a", "st1_b")
                if s == 3:
                    dve.wait_ge(S["x3_hi_ok"], b * T + 1)
                    V.scalar_tensor_tensor(x3_lo[:, 0, :], xres[:, 0, :], tail[:, 0:1], f32(x3_hi[:, 0, :]),
                                           ALU.mult, ALU.subtract).then_inc(S["x3_lo0"], 1)

            def graph(b, more):
                for s in range(T + 3):
                    if s < T:
                        dve.wait_ge(S["m0_psum"], b * T + s + 1)
                        V.scalar_tensor_tensor(row[:, s % R, :], sup[:, s, :], dis[:, s:s + 1], nt[s % 2][:],
                                               ALU.mult, ALU.add).then_inc(S["row0_ok"], 1)
                    if 0 <= s - 2 < T:
                        normalise(b, s - 2, 0, "pow0_ok", "x1_ok")
                    if 0 <= s - 1 < T:
                        row_stats(b, s - 1, "y0_ok", "st0_a")
                    if 0 <= s - 3 < T:
                        x1_low(b, s - 3)
                    if 0 <= s - 1 < T:
                        aggregate(b, s - 1, 0, "st0_a", "st0_b")
                        variance(b, s - 1, "st0_b", "var0_ok")
                z_low(b, 0)
                diag_low(b, 0)
                for s in range(TH + 1):
                    if s < TH:
                        row1(b, s)
                    else:
                        z_low(b, 1)
                        row1(b, TH)
                        row1(b, TH + 1)
                        if more:
                            a_low(b + 1, 0, 0)
                    chain(b, s)
                for n in range(TH + 2, T):
                    row1(b, n)
                for k in range(T + 2):
                    if more and k == 1:
                        degrees(b + 1)
                    if more:
                        prepare(b + 1, k, TH + 1 + k, begun=k == 0)
                    else:
                        chain(b, TH + 1 + k)
                    if k == 1:
                        diag_low(b, 1)

            def x1_low(b, n):
                dve.wait_ge(S["x1_hi_ok"], b * T + n + 1)
                V.tensor_tensor(x1_lo[:, n, :], xres[:, n, :], f32(x1_hi[:, n, :]), ALU.subtract)\
                    .then_inc(S["x1_lo_ok"], 1)

            def first_graph():
                def a_half(k, half, use):
                    cols = slice(half * H, (half + 1) * H)
                    dve.wait_ge(S["at_hi_ok"], half * T + k + 1)
                    V.tensor_tensor(at_lo[:, k, cols], first_ring[use % len(first_ring)][:], f32(at_hi[:, k, cols]), ALU.subtract)\
                        .then_inc(S["at_lo_ok"], 1)

                def support(k):
                    dve.wait_ge(S["sup_psum"], k + 1)
                    V.tensor_tensor(sup[:, k, :], nt[k % 2][:], b0_bc[:], ALU.add).then_inc(S["sup_ok"], 1)

                def scaled_low(n):
                    dve.wait_ge(S["mv_hi_ok"], n + 1)
                    V.scalar_tensor_tensor(mv0_lo[:, n * D:(n + 1) * D], sup[:, n, :], dis[:, n:n + 1],
                                           f32(mv0_hi[:, n * D:(n + 1) * D]), ALU.mult, ALU.subtract)\
                        .then_inc(S["mv_lo_ok"], 1)

                for k in range(T):
                    a_half(k, 0, 2 * k)
                    dve.wait_ge(S["xt_hi_ok"], k + 1)
                    V.tensor_tensor(xt_lo[:, k % 2], first_ring[(2 * k + 1) % 6][:, 0:D].rearrange("p (j c) -> p j c", j=DT),
                                    f32(xt_hi[:, k % 2]), ALU.subtract).then_inc(S["xt_lo_ok"], 1)
                    if k > 0:
                        support(k - 1)
                support(T - 1)
                degrees(0)
                for k in range(T):
                    a_half(k, 1, 2 * T + k)
                    if k >= 2:
                        scaled_low(k - 2)
                for n in range(T - 2, T):
                    scaled_low(n)

            first_graph()
            with dve.Fori(0, B - 1) as i:
                graph(i, True)
            graph(B - 1, False)

        @block.gpsimd
        def _(pool):
            G = nc.gpsimd
            pool.sem_inc(S["head_out"], 16)
            pool.sem_inc(S["mix_out"], 16)
            pool.sem_inc(S["x3_out"], 32)
            pool.wait_ge(S["setup_v"], 7)
            pool.wait_ge(S["setup_a"], 2)

            def inverse_roots(b):
                pool.wait_ge(S["deg_ok"], b + 1)
                G.tensor_tensor(dis[:], degs[:], minus_half[:], ALU.pow).then_inc(S["dis_pow"], 1)
                pool.wait_ge(S["dis_pow"], b + 1)
                G.tensor_tensor(dism[:], dis[:], masks[:, bass.ds(b * T, T)], ALU.mult).then_inc(S["dism_ok"], 1)

            def power(b, n, layer, var, done, also=None):
                pool.wait_ge(S[var], b * T + n + 1)
                cols = var_col(layer, n)
                if also:
                    pool.wait_ge(S[also], b * T + n + 2)
                    cols = slice(cols.start - 1, cols.stop)
                if layer:
                    G.tensor_tensor(var_eps[:, cols], mean_var[:, cols, 1], ln_eps[:, 0:cols.stop - cols.start], ALU.add)\
                        .then_inc(S["ve_ok"], 1)
                    pool.wait_ge(S["ve_ok"], b * (T + 1) + n + layer)
                G.tensor_tensor(rstd[:, cols], var_eps[:, cols], minus_half[:, 0:cols.stop - cols.start], ALU.pow)\
                    .then_inc(S[done], 1)

            def diagonal(b, half):
                his, los = diag_tiles(at_hi, half), diag_tiles(at_lo, half)
                for (hi, tiles), (lo, _) in zip(his, los):
                    last = G.tensor_tensor(diag[:, tiles, :], f32(hi), f32(lo), ALU.add)
                last.then_inc(S["diag_ok"], 1)
                pool.wait_ge(S["diag_ok"], b * 4 + 2 * half + 1)
                rows = slice(TH * half, TH * (half + 1))
                G.tensor_tensor(diag[:, rows, :], diag[:, rows, :], epsi[:].unsqueeze(1).broadcast_to([P, TH, P]),
                                ALU.add).then_inc(S["diag_ok"], 1)

            def residual1(b, n):
                pool.wait_ge(S["relu1_ok"], b * T + n + 1)
                G.tensor_tensor(xres[:, n, :], row[:, n % R, :], xres[:, n, :], ALU.add).then_inc(S["y1_ok"], 1)

            def chain(b, s):
                if 0 < s - 3 < T:
                    n = s - 3
                    pool.wait_ge(S["x3_hi_ok"], b * T + n + 1)
                    G.tensor_tensor(x3_lo[:, n, :], xres[:, n, :], f32(x3_hi[:, n, :]), ALU.subtract).then_inc(S["x3_lo_ok"], 1)
                if s == 1:
                    power(b, 0, 1, "st1_b", "pow_ok")
                elif 2 <= s <= T:
                    power(b, s - 2, 2, "st2_b", "pow_ok", "st1_b")
                elif s == T + 1:
                    power(b, T - 1, 2, "st2_b", "pow_ok")

            def graph(b, more):
                pool.wait_ge(S["x3_out"], b * 32 + 32)
                for s in range(T + 1):
                    if s < T:
                        pool.wait_ge(S["relu0_ok"], b * T + s + 1)
                        G.tensor_tensor(xres[:, s, :], row[:, s % R, :], x_in[:, s, :], ALU.add).then_inc(S["y0_ok"], 1)
                    if s > 0:
                        power(b, s - 1, 0, "var0_ok", "pow0_ok")
                    if s in (2, 4):
                        diagonal(b, s // 2 - 1)
                for s in range(TH + 1):
                    if s < TH:
                        residual1(b, s)
                    chain(b, s)
                for s in range(TH + 1, T + 3):
                    if s <= T:
                        residual1(b, s - 1)
                    chain(b, s)
                    if more and s == TH + 1:
                        inverse_roots(b + 1)

            inverse_roots(0)
            with pool.Fori(0, B - 1) as i:
                graph(i, True)
            graph(B - 1, False)


def group_tiles(B):
    tiles = []
    for g, per in enumerate((4, 8, 16, 16, 16)):
        per = min(per, B)
        tiles += [(g, b0, per) for b0 in range(0, B, per)]
    return tiles


def runs(nodes):
    out = []
    for i, n in enumerate(nodes):
        if out and out[-1][1] + out[-1][2] == n:
            out[-1][2] += 1
        else:
            out.append([i, n, 1])
    return out


def scatters(B):
    tiles = group_tiles(B)
    return [(t, u) for u, (h, c0, nc0) in enumerate(tiles) if h == 0
            for t, (g, b0, nb) in enumerate(tiles) if g > 0 and b0 <= c0 < b0 + nb]


def layout_constants(B):
    tiles = group_tiles(B)
    same = np.zeros((P, len(tiles), 16), np.float32)
    for t, (g, b0, nb) in enumerate(tiles):
        for r in range(len(GROUPS[g]) * nb):
            same[r, t, r % nb] = 1
    pairs = scatters(B)
    place = np.zeros((P, len(pairs), P), np.float32)
    for q, (t, u) in enumerate(pairs):
        (g, b0, nb), (_, c0, nc0) = tiles[t], tiles[u]
        for i, node in enumerate(GROUPS[g]):
            for c in range(nc0):
                place[i * nb + c0 + c - b0, q, node * nc0 + c] = 1
    return np.eye(P, dtype=np.float32), same, place


def layer2_preloads(sh, B, adj, x2head, w1, w2, same):
    tiles = group_tiles(B)

    def preload_weights(sp):
        half = w1.shape[1] * w1.shape[2] // P
        for g in range(4):
            for i, w in enumerate((w1, w2)):
                dst = sh.a_rows[:, (2 * g + i) * half:(2 * g + i + 1) * half]
                sp.dma_start(dst.rearrange("p (k o) -> p k o", k=w.shape[1] // P), w[g].rearrange("(k p) o -> p k o", p=P))\
                    .then_inc(sh.S[f"w_in{g}"], 16)
        sp.dma_start(sh.same[:], same).then_inc(sh.S["adj_in"], 16)
        for t, (g, b0, nb) in enumerate(tiles):
            for i, n, k in runs(GROUPS[g]):
                for j, m, kk in runs(GROUPS[g]):
                    sp.dma_start(sh.cadj[i * nb:(i + k) * nb, t, j:j + kk],
                                 adj[b0:b0 + nb, n:n + k, m:m + kk].rearrange("b i m -> i b m"),
                                 allow_slow_non_contiguous=True).then_inc(sh.S["adj_in"], 16)

    def preload_rows(sp):
        D = x2head.shape[2]
        for t, (g, b0, nb) in enumerate(tiles):
            for i, n, k in runs(GROUPS[g]):
                sp.dma_start(sh.x_rows[i * nb:(i + k) * nb, t * D:(t + 1) * D],
                             x2head[b0:b0 + nb, n:n + k, :].rearrange("b i d -> i b d")).then_inc(sh.S["rows_in"], 16)

    n_runs = [len(runs(GROUPS[g])) for g, _, _ in tiles]
    return preload_weights, preload_rows, 16 * (1 + sum(n * n for n in n_runs)), 16 * sum(n_runs)


def part2(nc, sh, adj_loaded, rows_loaded, B, w1, b1, w2, b2, fusion, place, x3, preload_part3, preload_nodes):
    G5, D, HID = w1.shape
    DT, HT = D // P, HID // P
    tiles = group_tiles(B)
    NT = len(tiles)
    rows = [len(GROUPS[g]) * nb for g, _, nb in tiles]
    NU = sum(g == 0 for g, _, _ in tiles)
    pairs = scatters(B)
    assert max(rows) <= P

    with ExitStack() as ctx:
        def sb(name, shape, dt=F32):
            return ctx.enter_context(nc.sbuf_tensor(name, shape, dt))

        def ps(name):
            return ctx.enter_context(nc.psum_tensor(name, [P, 512], F32))

        W = DT * HID
        WR = 6
        w_hi, w_lo = sb("w_hi", [P, WR, W], F32R), sb("w_lo", [P, WR, W], F32R)
        w_last = sb("w_last", [P, 2 * W])
        w_raw = [sh.a_rows[:, q * W:(q + 1) * W] for q in range(2 * G5 - 2)] + [w_last[:, 0:W], w_last[:, W:2 * W]]
        b1_bc, b2_bc = sb("g_b1", [P, G5, HID]), sb("g_b2", [P, G5, D])
        xg = sh.x_rows[:, 0:NT * D].rearrange("p (t d) -> p t d", t=NT)
        cadj, ident, same_sb = sh.cadj, sh.ident, sh.same
        bd = sb("bd", [P, NT, P])
        bt_hi, bt_lo = sb("bt_hi", [P, NT, P], F32R), sb("bt_lo", [P, NT, P], F32R)
        xt_hi, xt_lo = sb("g_xt_hi", [P, 2, DT, P], F32R), sb("g_xt_lo", [P, 2, DT, P], F32R)
        s1_hi, s1_lo = sb("s1_hi", [P, 2, HID], F32R), sb("s1_lo", [P, 2, HID], F32R)
        hid = sb("hid", [P, 2, HID])
        ht_hi, ht_lo = sb("ht_hi", [P, 2, HT, P], F32R), sb("ht_lo", [P, 2, HT, P], F32R)
        s2_hi, s2_lo = sb("s2_hi", [P, 2, D], F32R), sb("s2_lo", [P, 2, D], F32R)
        og = sb("og", [P, NT, D])
        place_sb = sb("place_sb", [P, len(pairs), P])
        deg, nonzero, dinv = sb("g_deg", [P, NT]), sb("g_nz", [P, NT]), sb("g_dinv", [P, NT])
        half = sb("g_half", [P, NT])
        fw, fmax, fsum = sb("fw", [P, G5]), sb("fmax", [P, 1]), sb("fsum", [P, 1])
        stats, mean_var = sb("g_stats", [P, NU, 6]), sb("g_mv", [P, NU, 2])
        var_eps, rstd = sb("g_ve", [P, NU]), sb("g_rstd", [P, NU])

        p_a, p_b, p_c, p_d, p_e, p_f = (ps(f"g_psum_{c}") for c in "abcdef")
        p_u = [ps(f"g_psum_u{i}") for i in range(2)]

        names = ["fw_in", "b1_in", "b2_in", "place_in", "w_in4", "w_hi_ok", "w_lo_ok", "prep", "bd_a", "bd_b", "bd_ok",
                 "deg_ok", "dinv_a", "dinv_ok", "fuse", "half_ok",
                 "a_psum", "a_hi_ok", "a_lo_ok", "b_psum", "b_hi_ok", "b_lo_ok", "c_psum", "c_ok", "c_relu",
                 "d_psum", "d_hi_ok", "d_lo_ok", "e_psum", "e_hi_ok", "e_lo_ok", "f_psum", "f_ok", "f_relu",
                 "u_psum", "u_a", "u_y", "u_st", "u_mv", "u_ve", "u_pow", "u_x"]
        S = {n: ctx.enter_context(nc.semaphore("p2_" + n)) for n in names}
        S.update(sh.S)
        of_group = {g: [t for t in range(NT) if tiles[t][0] == g] for g in range(G5)}
        latest = {2 * g + i: of_group[g][0] + 3 * i for g in range(G5) for i in range(2)}
        split_order = sorted(latest, key=latest.get)

        def splits_done(q):
            return split_order.index(q) + 1

        def slot(q):
            return split_order.index(q) % WR

        def last_user(q):
            return ("b_psum", "e_psum")[q % 2], of_group[q // 2][-1]

        split_steps = []
        for n, q in enumerate(split_order):
            step = min(n - 1, latest[q])
            if n >= WR:
                user, tile = last_user(split_order[n - WR])
                step = max(step, tile + {"b_psum": 1, "e_psum": 4}[user] + 1)
            split_steps.append(max([step] + split_steps[-1:]))
            assert split_steps[n] <= latest[q]
        splits_at = {s: [q for q, at in zip(split_order, split_steps) if at == s] for s in range(-1, NT + 6)}

        block = ctx.enter_context(nc.Block("part2"))

        @block.sync
        def _(sp):
            sp.dma_start(fw[:], fusion.unsqueeze(0).broadcast_to([P, G5])).then_inc(S["fw_in"], 16)
            sp.dma_start(b1_bc[:], b1.unsqueeze(0).broadcast_to([P, G5, HID])).then_inc(S["b1_in"], 16)
            sp.dma_start(b2_bc[:], b2.unsqueeze(0).broadcast_to([P, G5, D])).then_inc(S["b2_in"], 16)
            for i, w in enumerate((w1, w2)):
                sp.dma_start(w_last[:, i * W:(i + 1) * W].rearrange("p (k o) -> p k o", k=w.shape[1] // P),
                             w[G5 - 1].rearrange("(k p) o -> p k o", p=P)).then_inc(S["w_in4"], 16)
            sp.dma_start(place_sb[:], place).then_inc(S["place_in"], 16)
            preload_part3(sp)
            for u in range(NU):
                _, b0, nb = tiles[u]
                r = rows[u]
                sp.wait_ge(S["u_x"], u + 1)
                sp.dma_start(x3[b0:b0 + nb, 0:NODES, :].rearrange("b i d -> i b d"), xg[0:r, u, :])\
                    .then_inc(S[f"nodes_out{min(u, 1)}"], 16)
                if u == 0:
                    sp.wait_ge(S["nodes_out0"], 16)
                    preload_nodes(sp)

        @block.tensor
        def _(pe):
            T_ = nc.tensor

            def stage_a(t):
                r = rows[t]
                pe.wait_ge(S["bd_ok"], t + 1)
                if t == 0:
                    pe.wait_ge(S["rows_in"], rows_loaded)
                else:
                    pe.wait_ge(S["a_lo_ok"], 2 * t)
                for j in range(DT):
                    T_.transpose(p_a[:, j * P:j * P + r], xg[0:r, t, j * P:(j + 1) * P], ident[0:r, 0:r])
                T_.transpose(p_a[0:r, DT * P:DT * P + r], bd[0:r, t, 0:r], ident[0:r, 0:r]).then_inc(S["a_psum"], 1)

            def stage_b(t):
                g, r = tiles[t][0], rows[t]
                pe.wait_ge(S["w_lo_ok"], splits_done(2 * g))
                pe.wait_ge(S["a_lo_ok"], 2 * t + 2)
                if t > 0:
                    pe.wait_ge(S["b_lo_ok"], t)
                for j in range(DT):
                    last = split_matmuls(nc, p_b[0:r, :], xt_hi[:, t % 2, j, 0:r], xt_lo[:, t % 2, j, 0:r],
                                         w_hi[:, slot(2 * g), j * HID:(j + 1) * HID],
                                         w_lo[:, slot(2 * g), j * HID:(j + 1) * HID],
                                         j == 0, j == DT - 1)
                last.then_inc(S["b_psum"], 1)

            def stage_c(t):
                r = rows[t]
                pe.wait_ge(S["b_lo_ok"], t + 1)
                if t > 0:
                    pe.wait_ge(S["c_ok"], t)
                split_matmuls(nc, p_c[0:r, :], bt_hi[0:r, t, 0:r], bt_lo[0:r, t, 0:r], s1_hi[0:r, t % 2, :],
                              s1_lo[0:r, t % 2, :], True, True).then_inc(S["c_psum"], 1)

            def stage_d(t):
                r = rows[t]
                pe.wait_ge(S["c_relu"], t + 1)
                if t > 0:
                    pe.wait_ge(S["d_lo_ok"], t)
                for j in range(HT):
                    last = T_.transpose(p_d[:, j * P:j * P + r], hid[0:r, t % 2, j * P:(j + 1) * P], ident[0:r, 0:r])
                last.then_inc(S["d_psum"], 1)

            def stage_e(t):
                g, r = tiles[t][0], rows[t]
                pe.wait_ge(S["w_lo_ok"], splits_done(2 * g + 1))
                pe.wait_ge(S["d_lo_ok"], t + 1)
                if t > 0:
                    pe.wait_ge(S["e_lo_ok"], t)
                for j in range(HT):
                    last = split_matmuls(nc, p_e[0:r, 0:D], ht_hi[:, t % 2, j, 0:r], ht_lo[:, t % 2, j, 0:r],
                                         w_hi[:, slot(2 * g + 1), j * D:(j + 1) * D],
                                         w_lo[:, slot(2 * g + 1), j * D:(j + 1) * D],
                                         j == 0, j == HT - 1)
                last.then_inc(S["e_psum"], 1)

            def stage_f(t):
                r = rows[t]
                pe.wait_ge(S["e_lo_ok"], t + 1)
                if t > 0:
                    pe.wait_ge(S["f_ok"], t)
                split_matmuls(nc, p_f[0:r, 0:D], bt_hi[0:r, t, 0:r], bt_lo[0:r, t, 0:r], s2_hi[0:r, t % 2, :],
                              s2_lo[0:r, t % 2, :], True, True).then_inc(S["f_psum"], 1)

            def stage_g(t):
                for q, (v, u) in enumerate(pairs):
                    if v == t:
                        pe.wait_ge(S["place_in"], 16)
                        pe.wait_ge(S["f_relu"], t + 1)
                        of_u = [p for p, (_, w) in enumerate(pairs) if w == u]
                        last = T_.matmul(p_u[u // 2][0:rows[u], (u % 2) * D:(u % 2 + 1) * D],
                                         place_sb[0:rows[t], q, 0:rows[u]], og[0:rows[t], t, :],
                                         start=q == of_u[0] and u % 2 == 0, stop=q == of_u[-1], skip_group_check=True)
                        if q == of_u[-1]:
                            last.then_inc(S["u_psum"], 1)

            for s in range(NT + 6):
                for lag, stage in ((6, stage_g), (5, stage_f), (4, stage_e), (3, stage_d), (2, stage_c), (1, stage_b),
                                   (0, stage_a)):
                    if 0 <= s - lag < NT:
                        stage(s - lag)

        @block.scalar
        def _(act):
            A = nc.scalar.activation

            def fusion_exp():
                act.wait_ge(S["fuse"], 1)
                A(fw[:], fw[:], ACT.Exp, bias=fmax[:, 0:1], accum_out=fsum[:, 0:1]).then_inc(S["fuse"], 1)

            def weights_high(q):
                act.wait_ge(S[f"w_in{q // 2}"], 16 * 2)
                if splits_done(q) > WR:
                    user, tile = last_user(split_order[splits_done(q) - 1 - WR])
                    act.wait_ge(S[user], tile + 1)
                A(w_hi[:, slot(q), :], w_raw[q], ACT.Copy).then_inc(S["w_hi_ok"], 1)

            weights_high(*splits_at[-1])

            def stage_a(t):
                r = rows[t]
                act.wait_ge(S["a_psum"], t + 1)
                A(xt_hi[:, t % 2, :, 0:r], p_a[:, 0:DT * P].rearrange("p (j c) -> p j c", j=DT)[:, :, 0:r], ACT.Copy)\
                    .then_inc(S["a_hi_ok"], 1)
                A(bt_hi[0:r, t, 0:r], p_a[0:r, DT * P:DT * P + r], ACT.Copy).then_inc(S["a_hi_ok"], 1)

            def stage_b(t):
                r = rows[t]
                act.wait_ge(S["b_psum"], t + 1)
                if t == 0:
                    act.wait_ge(S["dinv_ok"], 1)
                A(s1_hi[0:r, t % 2, :], p_b[0:r, :], ACT.Copy, scale=dinv[0:r, t:t + 1]).then_inc(S["b_hi_ok"], 1)

            def stage_c(t):
                r = rows[t]
                act.wait_ge(S["c_ok"], t + 1)
                A(hid[0:r, t % 2, :], hid[0:r, t % 2, :], ACT.Relu).then_inc(S["c_relu"], 1)

            def stage_d(t):
                r = rows[t]
                act.wait_ge(S["d_psum"], t + 1)
                A(ht_hi[:, t % 2, :, 0:r], p_d[:].rearrange("p (j c) -> p j c", j=HT)[:, :, 0:r], ACT.Copy)\
                    .then_inc(S["d_hi_ok"], 1)

            def stage_e(t):
                r = rows[t]
                act.wait_ge(S["e_psum"], t + 1)
                A(s2_hi[0:r, t % 2, :], p_e[0:r, 0:D], ACT.Copy, scale=dinv[0:r, t:t + 1]).then_inc(S["e_hi_ok"], 1)

            def stage_f(t):
                g, r = tiles[t][0], rows[t]
                act.wait_ge(S["f_ok"], t + 1)
                if t == 0:
                    act.wait_ge(S["fuse"], 4)
                A(og[0:r, t, :], og[0:r, t, :], ACT.Relu, scale=fw[0:r, g:g + 1]).then_inc(S["f_relu"], 1)

            for s in range(NT + 5):
                for lag, stage in ((5, stage_f), (4, stage_e), (3, stage_d), (2, stage_c), (1, stage_b), (0, stage_a)):
                    if 0 <= s - lag < NT:
                        stage(s - lag)
                for q in splits_at[s]:
                    weights_high(q)
                if s == 2:
                    fusion_exp()

        @block.vector
        def _(dve):
            V = nc.vector
            dve.wait_ge(S["adj_in"], adj_loaded)
            V.memset(half[:], -0.5).then_inc(S["half_ok"], 1)
            V.memset(deg[:], 1.0).then_inc(S["prep"], 1)
            dve.wait_ge(S["prep"], 1)

            def fusion_max():
                dve.wait_ge(S["fw_in"], 16)
                V.tensor_reduce(fmax[:], fw[:], mybir.AxisListType.X, ALU.max, negate=True).then_inc(S["fuse"], 1)

            def fusion_weights():
                dve.wait_ge(S["fuse"], 2)
                V.reciprocal(fsum[:], fsum[:]).then_inc(S["fuse"], 1)
                dve.wait_ge(S["fuse"], 3)
                V.tensor_scalar(fw[:], fw[:], fsum[:, 0:1], None, ALU.mult).then_inc(S["fuse"], 1)

            for t, (g, b0, nb) in enumerate(tiles):
                n, r = len(GROUPS[g]), rows[t]
                V.tensor_tensor(bd[0:r, t, 0:r].rearrange("p (j b) -> p j b", b=nb),
                                cadj[0:r, t, 0:n].unsqueeze(2).broadcast_to([r, n, nb]),
                                same_sb[0:r, t, 0:nb].unsqueeze(1).broadcast_to([r, n, nb]), ALU.mult)\
                    .then_inc(S["bd_a"], 1)
            for t in range(NT):
                r = rows[t]
                dve.wait_ge(S["bd_a"], t + 1)
                V.tensor_tensor(bd[0:r, t, 0:r], bd[0:r, t, 0:r], ident[0:r, 0:r], ALU.add).then_inc(S["bd_ok"], 1)
            def degrees():
                for t in range(NT):
                    r = rows[t]
                    dve.wait_ge(S["bd_ok"], t + 1)
                    V.tensor_reduce(deg[0:r, t:t + 1], bd[0:r, t, 0:r], mybir.AxisListType.X, ALU.add).then_inc(S["bd_b"], 1)
                dve.wait_ge(S["bd_b"], NT)
                V.tensor_scalar(nonzero[:], deg[:], 0.0, None, ALU.not_equal).then_inc(S["deg_ok"], 1)
                V.scalar_tensor_tensor(dinv[:], deg[:], 0.0, deg[:], ALU.is_equal, ALU.add).then_inc(S["deg_ok"], 1)

            def weights_low(q):
                dve.wait_ge(S["w_hi_ok"], splits_done(q))
                V.tensor_tensor(w_lo[:, slot(q), :], w_raw[q], f32(w_hi[:, slot(q), :]), ALU.subtract).then_inc(S["w_lo_ok"], 1)

            weights_low(*splits_at[-1])

            def stage_a(t):
                r = rows[t]
                dve.wait_ge(S["a_hi_ok"], 2 * t + 2)
                V.tensor_tensor(xt_lo[:, t % 2, :, 0:r], p_a[:, 0:DT * P].rearrange("p (j c) -> p j c", j=DT)[:, :, 0:r],
                                f32(xt_hi[:, t % 2, :, 0:r]), ALU.subtract).then_inc(S["a_lo_ok"], 1)
                V.tensor_tensor(bt_lo[0:r, t, 0:r], p_a[0:r, DT * P:DT * P + r], f32(bt_hi[0:r, t, 0:r]), ALU.subtract)\
                    .then_inc(S["a_lo_ok"], 1)

            def stage_b(t):
                r = rows[t]
                dve.wait_ge(S["b_hi_ok"], t + 1)
                if t == 0:
                    dve.wait_ge(S["dinv_ok"], 1)
                V.scalar_tensor_tensor(s1_lo[0:r, t % 2, :], p_b[0:r, :], dinv[0:r, t:t + 1], f32(s1_hi[0:r, t % 2, :]),
                                       ALU.mult, ALU.subtract).then_inc(S["b_lo_ok"], 1)

            def stage_c(t):
                g, r = tiles[t][0], rows[t]
                dve.wait_ge(S["c_psum"], t + 1)
                if t == 0:
                    dve.wait_ge(S["b1_in"], 16)
                V.scalar_tensor_tensor(hid[0:r, t % 2, :], p_c[0:r, :], dinv[0:r, t:t + 1], b1_bc[0:r, g, :],
                                       ALU.mult, ALU.add).then_inc(S["c_ok"], 1)

            def stage_d(t):
                r = rows[t]
                dve.wait_ge(S["d_hi_ok"], t + 1)
                V.tensor_tensor(ht_lo[:, t % 2, :, 0:r], p_d[:].rearrange("p (j c) -> p j c", j=HT)[:, :, 0:r],
                                f32(ht_hi[:, t % 2, :, 0:r]), ALU.subtract).then_inc(S["d_lo_ok"], 1)

            def stage_e(t):
                r = rows[t]
                dve.wait_ge(S["e_hi_ok"], t + 1)
                V.scalar_tensor_tensor(s2_lo[0:r, t % 2, :], p_e[0:r, 0:D], dinv[0:r, t:t + 1], f32(s2_hi[0:r, t % 2, :]),
                                       ALU.mult, ALU.subtract).then_inc(S["e_lo_ok"], 1)

            def stage_f(t):
                g, r = tiles[t][0], rows[t]
                dve.wait_ge(S["f_psum"], t + 1)
                if t == 0:
                    dve.wait_ge(S["b2_in"], 16)
                V.scalar_tensor_tensor(og[0:r, t, :], p_f[0:r, 0:D], dinv[0:r, t:t + 1], b2_bc[0:r, g, :],
                                       ALU.mult, ALU.add).then_inc(S["f_ok"], 1)

            for s in range(NT + 5):
                for lag, stage in ((5, stage_f), (4, stage_e), (3, stage_d), (2, stage_c), (1, stage_b), (0, stage_a)):
                    if 0 <= s - lag < NT:
                        stage(s - lag)
                if s == 0:
                    degrees()
                for q in splits_at[s]:
                    weights_low(q)
                if s == 1:
                    fusion_max()
                if s == 3:
                    fusion_weights()
            def gather(u):
                r = rows[u]
                dve.wait_ge(S["u_psum"], min(NU, u - u % 2 + 2))
                dve.wait_ge(S["f_relu"], NT)
                V.tensor_tensor(og[0:r, u, :], p_u[u // 2][0:r, (u % 2) * D:(u % 2 + 1) * D], og[0:r, u, :], ALU.add)\
                    .then_inc(S["u_a"], 1)

            def residual(u):
                r = rows[u]
                dve.wait_ge(S["u_a"], u + 1)
                V.tensor_tensor(xg[0:r, u, :], xg[0:r, u, :], og[0:r, u, :], ALU.add).then_inc(S["u_y"], 1)

            def node_stats(u):
                r = rows[u]
                dve.wait_ge(S["u_y"], u + 1)
                V.bn_stats(stats[0:r, u, :], xg[0:r, u, :]).then_inc(S["u_st"], 1)

            def moments(u):
                r = rows[u]
                dve.wait_ge(S["u_st"], u + 1)
                V.bn_aggr(mean_var[0:r, u, :], stats[0:r, u, :]).then_inc(S["u_mv"], 1)

            def variance(u):
                r = rows[u]
                dve.wait_ge(S["u_mv"], u + 1)
                V.tensor_scalar(var_eps[0:r, u:u + 1], mean_var[0:r, u, 1:2], LN_EPS, None, ALU.add).then_inc(S["u_ve"], 1)

            def normalise(u):
                r = rows[u]
                dve.wait_ge(S["u_pow"], u + 1)
                V.tensor_scalar(xg[0:r, u, :], xg[0:r, u, :], mean_var[0:r, u, 0:1], rstd[0:r, u:u + 1],
                                ALU.subtract, ALU.mult).then_inc(S["u_x"], 1)

            for group in ([0], range(1, NU)):
                for stage in (gather, residual, node_stats, moments, variance):
                    for u in group:
                        stage(u)
                    if group and group[0] == 1 and stage is gather:
                        normalise(0)
            if NU == 1:
                normalise(0)
            for u in range(1, NU):
                normalise(u)

        @block.gpsimd
        def _(pool):
            G = nc.gpsimd
            pool.wait_ge(S["half_ok"], 1)
            pool.wait_ge(S["deg_ok"], 2)
            G.tensor_tensor(dinv[:], dinv[:], half[:], ALU.pow).then_inc(S["dinv_a"], 1)
            pool.wait_ge(S["dinv_a"], 1)
            G.tensor_tensor(dinv[:], dinv[:], nonzero[:], ALU.mult).then_inc(S["dinv_ok"], 1)
            for u in range(NU):
                r = rows[u]
                pool.wait_ge(S["u_ve"], u + 1)
                G.tensor_tensor(rstd[0:r, u:u + 1], var_eps[0:r, u:u + 1], half[0:r, 0:1], ALU.pow).then_inc(S["u_pow"], 1)


def open_part3(ctx, nc, sh, mixed, x3, near_at, v1, c1, rms_w, v2, c2):
    D, HID = v1.shape
    B, H = mixed.shape[0], mixed.shape[3]
    DT, KT = D // P, HID // P
    pre = Held()

    def sb(name, shape, dt=F32):
        return ctx.enter_context(nc.sbuf_tensor(name, shape, dt))

    pre.v1_raw, pre.v2_raw = sb("v1_raw", [P, DT, HID]), sb("v2_raw", [P, KT, D])
    pre.mix = sh.mix[:].rearrange("p (h j n) -> p h j n", h=2, j=DT)
    pre.near = sb("near", [P, 2 * H], F32R)
    pre.x_four = sb("x_four", [P, D])
    pre.cw_rows = sb("cw_rows", [2 * KT, P])
    pre.c2_bc = sb("c2_bc", [P, 2, D])
    names = ["v_in", "cw_ok", "v2_ok", "const_in", "setup_a", "setup_v", "setup_t", "mix_in0", "mix_in1", "near_in", "four_in", "near_hi_ok",
             "near_lo_ok", "xr_in0", "xr_in1",
             "corr_psum", "agg_ok", "agg_hi_ok", "agg_lo_ok", "hid_psum", "hb_ok", "sq_ok", "ss_ok",
             "sum_psum", "ms_ok", "rr_ok", "rr_hi_ok", "rr_lo_ok", "rd_ok", "rb_psum", "t_ok", "silu_ok", "s_hi_ok",
             "s_lo_ok", "o_step", "xb_ok", "y_ok", "st_ok", "mv_ok", "ve_ok", "pw_ok", "out_ok", "stored0", "stored1"]
    pre.S = S = {n: ctx.enter_context(nc.semaphore("p3_" + n)) for n in names}
    mix_v = mixed.rearrange("b p (j h) n -> b p h j n", h=2)

    def load_mix(sp, b, h):
        sp.dma_start(pre.mix[:, h], mix_v[b, :, h]).then_inc(S[f"mix_in{h}"], 16)

    def load_near(sp, b):
        for i in range(4):
            sp.dma_start(f32(pre.near[NEAR * i:NEAR * (i + 1), :]), near_at[b, i // 2]).then_inc(S["near_in"], 16)

    def load_four(sp, b):
        for i in range(4):
            sp.dma_start(pre.x_four[NEAR * i:NEAR * (i + 1), :], x3[b, 0:NEAR, :]).then_inc(S["four_in"], 16)

    def preload(sp):
        sp.dma_start(pre.v1_raw[:], v1.rearrange("(k p) n -> p k n", p=P)).then_inc(S["v_in"], 16)
        sp.dma_start(pre.v2_raw[:], v2.rearrange("(k p) n -> p k n", p=P)).then_inc(S["v_in"], 16)
        sp.dma_start(pre.cw_rows[0:KT, :], c1.rearrange("(k p) -> k p", p=P)).then_inc(S["const_in"], 16)
        sp.dma_start(pre.cw_rows[KT:2 * KT, :], rms_w.rearrange("(k p) -> k p", p=P)).then_inc(S["const_in"], 16)
        for i in range(2):
            sp.dma_start(pre.c2_bc[:, i, :], c2.rearrange("(a d) -> a d", a=1).broadcast_to([P, D])).then_inc(S["const_in"], 16)
        sp.wait_ge(sh.S["mix_out"], 16 * B + 16)
        load_mix(sp, 0, 0)
        load_mix(sp, 0, 1)
        load_near(sp, 0)

    pre.load_mix, pre.load_near, pre.load_four, pre.preload = load_mix, load_near, load_four, preload
    return pre


def part3(nc, sh, pre, mixed, x3, near_at, v1, v2, out):
    B, N, D = x3.shape
    HID = v1.shape[1]
    H = N // 2
    DT, KT, RT = D // P, HID // P, H // P
    assert 4 * NEAR == P
    LAG = 6
    SR = 4
    U = 2 * B

    with ExitStack() as ctx:
        def sb(name, shape, dt=F32):
            return ctx.enter_context(nc.sbuf_tensor(name, shape, dt))

        def ps(name):
            return ctx.enter_context(nc.psum_tensor(name, [P, 512], F32))

        v1_hi, v1_lo = sb("v1_hi", [P, DT, HID], F32R), sb("v1_lo", [P, DT, HID], F32R)
        v2_hi, v2_lo = sb("v2_hi", [P, KT, D], F32R), sb("v2_lo", [P, KT, D], F32R)
        mix, near, cw_rows, c2_bc, ident, S = pre.mix, pre.near, pre.cw_rows, pre.c2_bc, sh.ident, pre.S
        agg_hi, agg_lo = sb("agg_hi", [P, 2, DT, H], F32R), sb("agg_lo", [P, 2, DT, H], F32R)
        x_near, x_four = sb("x_near", [P, D], F32R), pre.x_four
        hb = sb("hb", [P, 2, KT, H])
        sq = sb("sq", [P, SR, H])
        ssum = sb("ssum", [P, 2, H])
        s_hi, s_lo = sb("s_hi", [P, SR, H], F32R), sb("s_lo", [P, SR, H], F32R)
        rd_hi, rd_lo = sb("rd_hi", [P, RT, P], F32R), sb("rd_lo", [P, RT, P], F32R)
        rr_hi, rr_lo = sb("rr_hi", [P, RT], F32R), sb("rr_lo", [P, RT], F32R)
        ones_r = sb("ones_r", [P, P], F32R)
        xr = sb("xr", [P, 2, RT, D])
        ones = sb("t_ones", [P, P])
        cw = sb("cw", [P, 2 * KT])
        ms, rr = sb("ms", [P, RT]), sb("rr", [P, RT])
        half, spacer = sb("t_half", [P, RT]), sb("t_spacer", [P, 1])
        stats, mean_var = sb("t_stats", [P, RT, 6]), sb("t_mv", [P, RT, 2])
        var_eps, rstd = sb("t_ve", [P, RT]), sb("t_rstd", [P, RT])
        hp = [ps(f"hp{i}") for i in range(2)]
        op = [[ps(f"op{i}{j}") for j in range(2)] for i in range(2)]
        cp, rb = ps("cp"), ps("rb")

        block = ctx.enter_context(nc.Block("part3"))

        x_v = x3.rearrange("b (h t p) d -> b h p t d", h=2, p=P)
        o_v = out.rearrange("b (h t p) d -> b h p t d", h=2, p=P)

        def back(unit, n):
            b, h = unit
            return (b - n // 2, h) if n % 2 == 0 else (b - (n + 1) // 2 + h, 1 - h)

        def upto(unit, per, count):
            b, h = unit
            return b * (2 * per) + (h * per + count)

        def wait(eng, name, value):
            if not isinstance(value, int) or value > 0:
                eng.wait_ge(S[name], value)

        def walk(eng, step):
            def units(b, cur=True, prev=((True,) * 3, (True,) * 3), nxt=(True, True), halves=2):
                for h in range(halves):
                    for j in range(KT):
                        step((b, h), j, cur, prev[h], nxt[h])

            units(0, prev=((False, False, False), (True, False, False)))
            units(1, prev=((True, True, False), (True, True, True)))
            with eng.Fori(2, B - 1) as b:
                units(b)
            units(B - 1, nxt=(True, False))
            units(B, cur=False, prev=((True, True, True), (False, True, True)), nxt=(False, False))
            units(B + 1, cur=False, prev=((False, False, True),), nxt=(False,), halves=1)

        def lagging(unit, j, lag, prev):
            n, k = (1, j - lag) if j >= lag else (2, j - lag + KT)
            return (back(unit, n), k) if prev[n - 1] else None

        @block.sync
        def _(sp):
            def load_rows(b, h):
                sp.dma_start(xr[:, h], x_v[b, h]).then_inc(S[f"xr_in{h}"], 16)

            others = sum(g == 0 for g, _, _ in group_tiles(B)) - 1
            if others:
                sp.wait_ge(sh.S["nodes_out1"], 16 * others)

            def store(b, h):
                sp.wait_ge(S["out_ok"], b * 2 + h + 1)
                sp.dma_start(o_v[b, h], xr[:, h]).then_inc(S[f"stored{h}"], 16)

            def graph(b, first, last):
                if not last:
                    sp.wait_ge(S["near_lo_ok"], b + 1)
                    pre.load_four(sp, b + 1)
                    for h in range(2):
                        sp.wait_ge(S["agg_lo_ok"], b * 4 + 2 * h + 2)
                        pre.load_mix(sp, b + 1, h)
                    pre.load_near(sp, b + 1)
                for h in range(2):
                    if not first:
                        store(b - 1, h)
                        sp.wait_ge(S[f"stored{h}"], b * 16)
                    load_rows(b, h)

            graph(0, True, False)
            with sp.Fori(1, B - 1) as i:
                graph(i, False, False)
            graph(B - 1, False, True)
            for h in range(2):
                store(B - 1, h)
            for h in range(2):
                sp.wait_ge(S[f"stored{h}"], 16 * B)

        @block.tensor
        def _(pe):
            T_ = nc.tensor
            pe.wait_ge(S["const_in"], 16 * 4)
            T_.transpose(cp[:, 0:2 * KT], cw_rows[:], ident[0:2 * KT, 0:2 * KT]).then_inc(S["setup_t"], 1)

            def correct(unit, j):
                b, h = unit
                if j == 0:
                    pe.wait_ge(S["cw_ok"], 1)
                    if h == 0:
                        pe.wait_ge(S["near_in"], b * 64 + 64)
                        pe.wait_ge(S["near_lo_ok"], b + 1)
                    wait(pe, "agg_ok", upto(back(unit, 1), 2, 2))
                    wait(pe, "ms_ok", upto(back(unit, 2), 1, 1))
                else:
                    pe.wait_ge(S["agg_ok"], upto(unit, 2, 1))
                T_.matmul(cp[:], x_near[:, j * P:(j + 1) * P], near[:, h * H:(h + 1) * H], start=True, stop=True)\
                    .then_inc(S["corr_psum"], 1)

            def hidden(unit, t):
                h = unit[1]
                if t == 0:
                    pe.wait_ge(S["agg_lo_ok"], upto(unit, 2, 2))
                    pe.wait_ge(S["setup_v"], 3 + DT)
                wait(pe, "hb_ok", upto(unit, KT, t - 1))
                cols = slice(t * P, (t + 1) * P)
                for j in range(DT):
                    last = split_matmuls(nc, hp[t % 2][:], v1_hi[:, j, cols], v1_lo[:, j, cols],
                                         agg_hi[:, h, j, :], agg_lo[:, h, j, :], j == 0, j == DT - 1)
                last.then_inc(S["hid_psum"], 1)

            def sums(unit, next_too):
                pe.wait_ge(S["ss_ok"], upto(unit, KT - 1, KT - 1))
                pe.wait_ge(S["agg_ok"], upto(back(unit, -1) if next_too else unit, 2, 2))
                for r in range(RT):
                    last = T_.matmul(cp[:, r:r + 1], ssum[:, unit[1], r * P:(r + 1) * P], ones[:, 0:1], start=True, stop=True)
                last.then_inc(S["sum_psum"], 1)

            def spread(unit):
                pe.wait_ge(S["rd_ok"], upto(unit, 1, 1))
                wait(pe, "t_ok", upto(back(unit, 1), KT, KT))
                T_.matmul(rb[:], ones_r[:], rd_hi[:].rearrange("p r c -> p (r c)"), start=True, stop=False)
                T_.matmul(rb[:], ones_r[:], rd_lo[:].rearrange("p r c -> p (r c)"), start=False, stop=True)\
                    .then_inc(S["rb_psum"], 1)

            def output(unit, k):
                h = unit[1]
                pe.wait_ge(S["s_lo_ok"], upto(unit, KT, k + 1))
                if k == 0:
                    pe.wait_ge(S["v2_ok"], 1)
                    wait(pe, "y_ok", upto(back(unit, 2), 2, 2))
                for r in range(RT):
                    cols = slice(r * P, (r + 1) * P)
                    last = split_matmuls(nc, op[h][r // 2][:, (r % 2) * D:(r % 2 + 1) * D],
                                         s_hi[:, k % SR, cols], s_lo[:, k % SR, cols], v2_hi[:, k, :], v2_lo[:, k, :],
                                         k == 0 and r % 2 == 0, k == KT - 1, group=False)
                last.then_inc(S["o_step"], 1)

            def step(unit, j, cur, prev, nxt):
                if cur:
                    hidden(unit, j)
                if prev[0] and j == 1:
                    sums(back(unit, 1), cur)
                if late := lagging(unit, j, LAG, prev):
                    output(*late)
                if prev[0] and j == 3:
                    spread(back(unit, 1))
                if nxt and j in (3, 4):
                    correct(back(unit, -1), j - 3)

            correct((0, 0), 0)
            correct((0, 0), 1)
            walk(pe, step)

        @block.scalar
        def _(act):
            A = nc.scalar.activation
            def near_high(b):
                act.wait_ge(S["four_in"], b * 64 + 64)
                wait(act, "corr_psum", upto((b - 1, 1), 2, 2))
                A(x_near[:], x_four[:], ACT.Copy).then_inc(S["near_hi_ok"], 1)

            near_high(0)
            act.wait_ge(S["v_in"], 16 * 2)
            for j in range(DT):
                A(v1_hi[:, j, :], pre.v1_raw[:, j, :], ACT.Copy).then_inc(S["setup_a"], 1)
            A(v2_hi[:], pre.v2_raw[:], ACT.Copy).then_inc(S["setup_a"], 1)
            act.wait_ge(S["cw_ok"], 1)

            def hidden(unit, t):
                h = unit[1]
                act.wait_ge(S["hid_psum"], upto(unit, KT, t + 1))
                A(hb[:, h, t, :], hp[t % 2][:], ACT.Identity, bias=cw[:, t:t + 1]).then_inc(S["hb_ok"], 1)
                wait(act, "ss_ok", upto(unit, KT - 1, t - SR) if t > SR else
                     upto(unit, KT - 1, 1) if t == SR else upto(back(unit, 1), KT - 1, t + KT - SR))
                act.wait_ge(S["hb_ok"], upto(unit, KT, t + 1))
                A(sq[:, t % SR, :], hb[:, h, t, :], ACT.Square).then_inc(S["sq_ok"], 1)

            def silu(unit, k):
                h = unit[1]
                act.wait_ge(S["t_ok"], upto(unit, KT, k + 1))
                A(hb[:, h, k, :], hb[:, h, k, :], ACT.Silu, scale=cw[:, KT + k:KT + k + 1]).then_inc(S["silu_ok"], 1)
                wait(act, "o_step", upto(unit, KT, k + 1 - SR))
                act.wait_ge(S["silu_ok"], upto(unit, KT, k + 1))
                A(s_hi[:, k % SR, :], hb[:, h, k, :], ACT.Copy).then_inc(S["s_hi_ok"], 1)

            def step(unit, j, cur, prev, nxt):
                if nxt and j == 2 and unit[1] == 1:
                    near_high(unit[0] + 1)
                if late := lagging(unit, j, LAG - 1, prev):
                    silu(*late)
                if cur:
                    hidden(unit, j)

            walk(act, step)

        @block.vector
        def _(dve):
            V = nc.vector
            V.memset(half[:], -0.5).then_inc(S["setup_v"], 1)
            V.memset(ones[:], 1.0).then_inc(S["setup_v"], 1)
            dve.wait_ge(S["setup_v"], 2)
            V.tensor_copy(ones_r[:], ones[:]).then_inc(S["setup_v"], 1)
            dve.wait_ge(S["setup_t"], 1)
            V.tensor_copy(cw[:], cp[:, 0:2 * KT]).then_inc(S["cw_ok"], 1)

            def split_v1(j):
                dve.wait_ge(S["setup_a"], j + 1)
                V.tensor_tensor(v1_lo[:, j, :], pre.v1_raw[:, j, :], f32(v1_hi[:, j, :]), ALU.subtract)\
                    .then_inc(S["setup_v"], 1)

            def split_v2():
                dve.wait_ge(S["setup_a"], DT + 1)
                V.tensor_tensor(v2_lo[:], pre.v2_raw[:], f32(v2_hi[:]), ALU.subtract).then_inc(S["v2_ok"], 1)

            def aggregate(unit, j):
                b, h = unit
                if j == 0:
                    dve.wait_ge(S[f"mix_in{h}"], b * 16 + 16)
                dve.wait_ge(S["corr_psum"], upto(unit, 2, j + 1))
                V.tensor_tensor(mix[:, h, j, :], cp[:], mix[:, h, j, :], ALU.add).then_inc(S["agg_ok"], 1)
                dve.wait_ge(S["agg_ok"], upto(unit, 2, j + 1))
                V.tensor_copy(agg_hi[:, h, j, :], mix[:, h, j, :]).then_inc(S["agg_hi_ok"], 1)

            def mean_square(unit):
                dve.wait_ge(S["sum_psum"], upto(unit, 1, 1))
                V.tensor_scalar(ms[:], cp[:, 0:RT], 1.0 / HID, RMS_EPS, ALU.mult, ALU.add).then_inc(S["ms_ok"], 1)

            def diagonals(unit):
                dve.wait_ge(S["rr_ok"], upto(unit, 1, 1))
                V.tensor_copy(rr_hi[:], rr[:]).then_inc(S["rr_hi_ok"], 1)
                dve.wait_ge(S["rr_hi_ok"], upto(unit, 1, 1))
                V.tensor_tensor(rr_lo[:], rr[:], f32(rr_hi[:]), ALU.subtract).then_inc(S["rr_lo_ok"], 1)
                dve.wait_ge(S["rr_lo_ok"], upto(unit, 1, 1))
                diagonal = ident[:].unsqueeze(1).broadcast_to([P, RT, P])
                for rd, part in ((rd_hi, rr_hi), (rd_lo, rr_lo)):
                    last = V.tensor_tensor(rd[:], f32(part[:]).unsqueeze(2).broadcast_to([P, RT, P]), diagonal, ALU.mult)
                last.then_inc(S["rd_ok"], 1)

            def scale(unit, k):
                h = unit[1]
                if k == 0:
                    dve.wait_ge(S["rb_psum"], upto(unit, 1, 1))
                    dve.wait_ge(S["sq_ok"], upto(unit, KT, KT))
                V.tensor_tensor(hb[:, h, k, :], rb[:], hb[:, h, k, :], ALU.mult).then_inc(S["t_ok"], 1)

            def silu_low(unit, k):
                dve.wait_ge(S["s_hi_ok"], upto(unit, KT, k + 1))
                V.tensor_tensor(s_lo[:, k % SR, :], hb[:, unit[1], k, :], f32(s_hi[:, k % SR, :]), ALU.subtract)\
                    .then_inc(S["s_lo_ok"], 1)

            def residual(unit):
                h = unit[1]
                dve.wait_ge(S["o_step"], upto(unit, KT, KT))
                dve.wait_ge(S["xb_ok"], upto(unit, 2, 2))
                for i in range(2):
                    rows = xr[:, h, 2 * i:2 * i + 2, :].rearrange("p r d -> p (r d)")
                    V.tensor_tensor(rows, op[h][i][:], rows, ALU.add).then_inc(S["y_ok"], 1)

            def row_stats(unit):
                h = unit[1]
                for r in range(RT):
                    if r % 2 == 0:
                        dve.wait_ge(S["y_ok"], upto(unit, 2, r // 2 + 1))
                    last = V.bn_stats(stats[:, r, :], xr[:, h, r, :])
                last.then_inc(S["st_ok"], 1)

            def variances(unit):
                dve.wait_ge(S["st_ok"], upto(unit, 1, 1))
                V.memset(spacer[:], 0.0)
                for r in range(RT):
                    last = V.bn_aggr(mean_var[:, r, :], stats[:, r, :])
                last.then_inc(S["mv_ok"], 1)
                dve.wait_ge(S["mv_ok"], upto(unit, 1, 1))
                V.tensor_scalar(var_eps[:], mean_var[:, :, 1], LN_EPS, None, ALU.add).then_inc(S["ve_ok"], 1)

            def normalise(unit):
                h = unit[1]
                dve.wait_ge(S["pw_ok"], upto(unit, 1, 1))
                for r in range(RT):
                    last = V.tensor_scalar(xr[:, h, r, :], xr[:, h, r, :], mean_var[:, r, 0:1], rstd[:, r:r + 1],
                                           ALU.subtract, ALU.mult)
                last.then_inc(S["out_ok"], 1)

            def near_low(b):
                dve.wait_ge(S["near_hi_ok"], b + 1)
                for i in (1, 3):
                    part = slice(NEAR * i, NEAR * (i + 1))
                    last = V.tensor_tensor(x_near[part, :], x_four[part, :], f32(x_near[part, :]), ALU.subtract)
                last.then_inc(S["near_lo_ok"], 1)

            def step(unit, j, cur, prev, nxt):
                if late := lagging(unit, j, LAG, prev):
                    silu_low(*late)
                if late := lagging(unit, j, LAG - 2, prev):
                    scale(*late)
                if prev[0] and j == 2:
                    mean_square(back(unit, 1))
                if prev[0] and j == 3:
                    diagonals(back(unit, 1))
                if nxt and j == 2 and unit[1] == 1:
                    near_low(unit[0] + 1)
                if nxt and j in (4, 5):
                    aggregate(back(unit, -1), j - 4)
                if prev[1] and j == 6:
                    residual(back(unit, 2))
                if prev[1] and j == 7:
                    row_stats(back(unit, 2))
                if prev[2] and j == 0:
                    variances(back(unit, 3))
                if prev[2] and j == 1:
                    normalise(back(unit, 3))

            near_low(0)
            split_v1(0)
            aggregate((0, 0), 0)
            split_v1(1)
            aggregate((0, 0), 1)
            split_v2()
            walk(dve, step)

        @block.gpsimd
        def _(pool):
            G = nc.gpsimd
            pool.wait_ge(S["setup_v"], 3)

            def agg_low(unit, j):
                h = unit[1]
                pool.wait_ge(S["agg_hi_ok"], upto(unit, 2, j + 1))
                G.tensor_tensor(agg_lo[:, h, j, :], mix[:, h, j, :], f32(agg_hi[:, h, j, :]), ALU.subtract)\
                    .then_inc(S["agg_lo_ok"], 1)

            def add_squares(unit, t):
                h = unit[1]
                pool.wait_ge(S["sq_ok"], upto(unit, KT, t + 1))
                if t > 1:
                    pool.wait_ge(S["ss_ok"], upto(unit, KT - 1, t - 1))
                G.tensor_tensor(ssum[:, h, :], sq[:, 0, :] if t == 1 else ssum[:, h, :], sq[:, t % SR, :], ALU.add)\
                    .then_inc(S["ss_ok"], 1)

            def inverse_rms(unit):
                pool.wait_ge(S["ms_ok"], upto(unit, 1, 1))
                G.tensor_tensor(rr[:], ms[:], half[:], ALU.pow).then_inc(S["rr_ok"], 1)

            def add_bias(unit, i):
                b, h = unit
                if i == 0:
                    pool.wait_ge(S[f"xr_in{h}"], b * 16 + 16)
                rows = xr[:, h, 2 * i:2 * i + 2, :]
                G.tensor_tensor(rows, rows, c2_bc[:], ALU.add).then_inc(S["xb_ok"], 1)

            def inverse_deviation(unit):
                pool.wait_ge(S["ve_ok"], upto(unit, 1, 1))
                G.tensor_tensor(rstd[:], var_eps[:], half[:], ALU.pow).then_inc(S["pw_ok"], 1)

            def step(unit, j, cur, prev, nxt):
                if prev[0] and j == 2:
                    inverse_rms(back(unit, 1))
                if prev[2] and j == 0:
                    inverse_deviation(back(unit, 3))
                if nxt and j in (5, 6):
                    agg_low(back(unit, -1), j - 5)
                if cur and j > 0:
                    add_squares(unit, j)
                if prev[1] and j in (2, 3):
                    add_bias(back(unit, 2), j - 2)

            agg_low((0, 0), 0)
            agg_low((0, 0), 1)
            walk(pool, step)


def program(nc, x, adj, nodemask, w0t, b0, w1, b1, g_w1, g_b1, g_w2, g_b2, fusion, eps, v1, c1, rms_w, v2, c2,
            eye, same, place, out):
    B, N, D = x.shape
    mixed = nc.dram_tensor("mixed_scratch", (B, P, 4, N // 2), F32).ap()
    x3 = nc.dram_tensor("x3_scratch", (B, N, D), F32).ap()
    near_at = nc.dram_tensor("near_scratch", (B, 2, NEAR, N), F32).ap()
    x2head = nc.dram_tensor("x2head_scratch", (B, NODES, D), F32).ap()
    with ExitStack() as ctx:
        sh = open_shared(ctx, nc, B, N, D)
        preload_weights, preload_rows, adj_loaded, rows_loaded = layer2_preloads(sh, B, adj, x2head, g_w1, g_w2, same)
        part1(nc, sh, x, adj, nodemask, w0t, b0, w1, b1, eps, eye, mixed, x3, near_at, x2head, preload_weights, preload_rows)
        pre = open_part3(ctx, nc, sh, mixed, x3, near_at, v1, c1, rms_w, v2, c2)
        part2(nc, sh, adj_loaded, rows_loaded, B, g_w1, g_b1, g_w2, g_b2, fusion, place, x3, pre.preload, lambda sp: pre.load_four(sp, 0))
        part3(nc, sh, pre, mixed, x3, near_at, v1, v2, out)


def kernel(x, adj, nodemask, L0_gnn_W, L0_gnn_b, L1_gnn_weight, L1_gnn_bias, L2_gnn_W1, L2_gnn_b1, L2_gnn_W2,
           L2_gnn_b2, L2_gnn_fusion_w, L3_gnn_epsilon, L3_gnn_W1, L3_gnn_b1, L3_gnn_rms_weight, L3_gnn_W2, L3_gnn_b2):
    import concourse.bacc as bacc
    from concourse.bass_utils import run_bass_kernel_spmd

    eye, same, place = layout_constants(x.shape[0])
    arrays = {
        "x": x, "adj": adj, "nodemask": nodemask, "w0t": np.asarray(L0_gnn_W).T, "b0": L0_gnn_b,
        "w1": L1_gnn_weight, "b1": L1_gnn_bias, "g_w1": L2_gnn_W1, "g_b1": L2_gnn_b1, "g_w2": L2_gnn_W2,
        "g_b2": L2_gnn_b2, "fusion": L2_gnn_fusion_w, "eps": np.asarray(L3_gnn_epsilon).reshape(1),
        "v1": L3_gnn_W1, "c1": L3_gnn_b1, "rms_w": L3_gnn_rms_weight, "v2": L3_gnn_W2, "c2": L3_gnn_b2,
        "eye": eye, "same": same, "place": place,
    }
    arrays = {n: np.ascontiguousarray(a) for n, a in arrays.items()}
    nc = bacc.Bacc("TRN2", target_bir_lowering=False, num_devices=1)
    args = {n: nc.dram_tensor("in_" + n, a.shape, F32, kind="ExternalInput").ap() for n, a in arrays.items()}
    out = nc.dram_tensor("out", x.shape, F32, kind="ExternalOutput").ap()
    program(nc, **args, out=out)
    r = run_bass_kernel_spmd(nc, [{"in_" + n: a for n, a in arrays.items()}], core_ids=[0])
    return r.results[0]["out"]
```
